# Optimizing a Trainium2 kernel written in Bass

```python
import numpy as np
import jax
import jax.numpy as jnp

def _softmax(x, axis=-1):
    return jax.nn.softmax(x, axis=axis)

def _gelu(x):
    return jax.nn.gelu(x, approximate=True)

def _silu(x):
    return jax.nn.silu(x)

def _sigmoid(x):
    return jax.nn.sigmoid(x)

def _layernorm(x, axis=-1, eps=1e-05):
    m = jnp.mean(x, axis=axis, keepdims=True)
    v = jnp.var(x, axis=axis, keepdims=True)
    return (x - m) / jnp.sqrt(v + eps)

def _scatter_add(tgt, idx, src, axis=0):
    return tgt.at[idx].add(src)

def _segment_sum(src, seg, n):
    return jax.ops.segment_sum(src, seg, n)
kernel_name = 'mk_seq_postln_d1_jaxref_r8_3449e5'

def setup_inputs(seed: int=0):
    np.random.seed(seed)
    _w = jnp.asarray

    def _L0_attn_setup():
        import jax, jax.numpy as jnp
        import numpy as np
        import math
        N_EMBD = 256
        N_HEAD = 16
        RATIO_KV = 4
        N_HEAD_KV = N_HEAD // RATIO_KV
        HEAD_DIM = N_EMBD // N_HEAD

        def alibi_slopes(n_heads):

            def pow2_slopes(n):
                start = 2 ** (-2 ** (-(math.log2(n) - 3)))
                return [start * start ** i for i in range(n)]
            if math.log2(n_heads).is_integer():
                return jnp.array(pow2_slopes(n_heads), dtype=jnp.float32)
            cp2 = 2 ** math.floor(math.log2(n_heads))
            base = pow2_slopes(cp2)
            if n_heads <= 2 * cp2:
                s = base + base[0::2]
            else:
                s = base + base[0::2] + base[1::2]
            return jnp.array(s[:n_heads], dtype=jnp.float32)
        key = jax.random.key(seed)
        ks = jax.random.split(key, 5)
        B, T = (4, 256)
        scale = 1.0 / math.sqrt(N_EMBD)
        x = jax.random.normal(ks[0], (B, T, N_EMBD), dtype=jnp.float32)
        Wq = jax.random.normal(ks[1], (N_EMBD, N_EMBD), dtype=jnp.float32) * scale
        Wk = jax.random.normal(ks[2], (N_EMBD, N_HEAD_KV * HEAD_DIM), dtype=jnp.float32) * scale
        Wv = jax.random.normal(ks[3], (N_EMBD, N_HEAD_KV * HEAD_DIM), dtype=jnp.float32) * scale
        Wo = jax.random.normal(ks[4], (N_EMBD, N_EMBD), dtype=jnp.float32) * scale
        return {'x': x, 'Wq': Wq, 'Wk': Wk, 'Wv': Wv, 'Wo': Wo}
    _L0_attn_in = _L0_attn_setup()

    def _L0_ffn_setup():
        import jax, jax.numpy as jnp
        import numpy as np
        E, H, I = (8, 256, 512)
        TOP_K = 1
        B, S = (1, 256)
        key = jax.random.key(seed)
        ks = jax.random.split(key, 7)
        std = 0.02
        return {'hidden_states': jax.random.normal(ks[0], (B, S, H), dtype=jnp.float32), 'router_w': jax.random.normal(ks[1], (E, H), dtype=jnp.float32) * std, 'gate_up_proj': jax.random.normal(ks[2], (E, H, 2 * I), dtype=jnp.float32) * std, 'down_proj': jax.random.normal(ks[3], (E, I, H), dtype=jnp.float32) * std, 'shared_gate_w': jax.random.normal(ks[4], (H, I), dtype=jnp.float32) * std, 'shared_up_w': jax.random.normal(ks[5], (H, I), dtype=jnp.float32) * std, 'shared_down_w': jax.random.normal(ks[6], (I, H), dtype=jnp.float32) * std}
    _L0_ffn_in = _L0_ffn_setup()
    _d = {'L0_attn_x': _L0_attn_in['x'], 'L0_attn_Wq': _L0_attn_in['Wq'], 'L0_attn_Wk': _L0_attn_in['Wk'], 'L0_attn_Wv': _L0_attn_in['Wv'], 'L0_attn_Wo': _L0_attn_in['Wo'], 'L0_ffn_router_w': _L0_ffn_in['router_w'], 'L0_ffn_gate_up_proj': _L0_ffn_in['gate_up_proj'], 'L0_ffn_down_proj': _L0_ffn_in['down_proj'], 'L0_ffn_shared_gate_w': _L0_ffn_in['shared_gate_w'], 'L0_ffn_shared_up_w': _L0_ffn_in['shared_up_w'], 'L0_ffn_shared_down_w': _L0_ffn_in['shared_down_w']}
    _x0 = _d['L0_attn_x']
    _d['L0_attn_x'] = jax.random.normal(jax.random.fold_in(jax.random.key(seed), 1), (2, 1024, 256), dtype=_x0.dtype)
    del _x0
    return _d

def reference(L0_attn_x, L0_attn_Wq, L0_attn_Wk, L0_attn_Wv, L0_attn_Wo, L0_ffn_router_w, L0_ffn_gate_up_proj, L0_ffn_down_proj, L0_ffn_shared_gate_w, L0_ffn_shared_up_w, L0_ffn_shared_down_w):

    def _L0_attn_ref(x, Wq, Wk, Wv, Wo):
        import jax, jax.numpy as jnp
        import numpy as np
        import math
        N_EMBD = 256
        N_HEAD = 16
        RATIO_KV = 4
        N_HEAD_KV = N_HEAD // RATIO_KV
        HEAD_DIM = N_EMBD // N_HEAD

        def alibi_slopes(n_heads):

            def pow2_slopes(n):
                start = 2 ** (-2 ** (-(math.log2(n) - 3)))
                return [start * start ** i for i in range(n)]
            if math.log2(n_heads).is_integer():
                return jnp.array(pow2_slopes(n_heads), dtype=jnp.float32)
            cp2 = 2 ** math.floor(math.log2(n_heads))
            base = pow2_slopes(cp2)
            if n_heads <= 2 * cp2:
                s = base + base[0::2]
            else:
                s = base + base[0::2] + base[1::2]
            return jnp.array(s[:n_heads], dtype=jnp.float32)
        B, T, C = x.shape
        rep = N_HEAD // N_HEAD_KV
        q = (x @ Wq).reshape(B, T, N_HEAD, HEAD_DIM).transpose(0, 2, 1, 3)
        k = (x @ Wk).reshape(B, T, N_HEAD_KV, HEAD_DIM).transpose(0, 2, 1, 3)
        v = (x @ Wv).reshape(B, T, N_HEAD_KV, HEAD_DIM).transpose(0, 2, 1, 3)
        k = jnp.repeat(k, rep, axis=1)
        v = jnp.repeat(v, rep, axis=1)
        scale = 1.0 / math.sqrt(HEAD_DIM)
        att = jnp.einsum('bhqd,bhkd->bhqk', q, k) * scale
        slopes = alibi_slopes(N_HEAD)
        pos = jnp.arange(T)
        rel = pos[None, :] - pos[:, None]
        alibi = slopes[:, None, None] * rel[None, :, :].astype(jnp.float32)
        alibi = jnp.repeat(alibi, rep, axis=0)[:N_HEAD]
        att = att + alibi[None]
        causal = jnp.triu(jnp.full((T, T), -jnp.inf, dtype=jnp.float32), k=1)
        att = att + causal[None, None]
        att = jax.nn.softmax(att.astype(jnp.float32), axis=-1).astype(q.dtype)
        y = jnp.einsum('bhqk,bhkd->bhqd', att, v)
        y = y.transpose(0, 2, 1, 3).reshape(B, T, C)
        return y @ Wo

    def _L0_ffn_ref(hidden_states, router_w, gate_up_proj, down_proj, shared_gate_w, shared_up_w, shared_down_w):
        import jax, jax.numpy as jnp
        import numpy as np
        E, H, I = (8, 256, 512)
        TOP_K = 1
        B, S = (1, 256)
        orig_shape = hidden_states.shape
        x = hidden_states.reshape(-1, H)
        T = x.shape[0]
        logits = x @ router_w.T
        top_vals, top_idx = jax.lax.top_k(logits, TOP_K)
        scores = jnp.full_like(logits, -jnp.inf)
        scores = scores.at[jnp.arange(T)[:, None], top_idx].set(top_vals)
        scores = jax.nn.sigmoid(scores.astype(jnp.float32)).astype(logits.dtype)
        xr = x[None, :, :] * scores.T[:, :, None]
        gate_up = jnp.einsum('eth,ehf->etf', xr, gate_up_proj)
        gate, up = jnp.split(gate_up, 2, axis=-1)
        routed = jnp.einsum('etf,efh->eth', up * jax.nn.silu(gate), down_proj)
        routed_sum = routed.sum(axis=0)
        shared = jax.nn.silu(x @ shared_gate_w) * (x @ shared_up_w) @ shared_down_w
        return (shared + routed_sum).reshape(orig_shape)
    x = L0_attn_x
    x = _layernorm(x + _L0_attn_ref(x, L0_attn_Wq, L0_attn_Wk, L0_attn_Wv, L0_attn_Wo), axis=-1)
    x = _layernorm(x + _L0_ffn_ref(x, L0_ffn_router_w, L0_ffn_gate_up_proj, L0_ffn_down_proj, L0_ffn_shared_gate_w, L0_ffn_shared_up_w, L0_ffn_shared_down_w), axis=-1)
    return x

_drawn_inputs = setup_inputs


def setup_inputs(seed=0):
    import zlib

    import numpy as np

    out = dict(_drawn_inputs(seed))
    spreads = {}
    factors = {'L0_ffn_router_w': 6.582,
     'L0_ffn_gate_up_proj': 6.186,
     'L0_ffn_down_proj': 6.175,
     'L0_ffn_shared_gate_w': 8.0,
     'L0_ffn_shared_up_w': 8.0,
     'L0_ffn_shared_down_w': 8.0}
    for name, (base, spread) in spreads.items():
        noise = np.random.default_rng([zlib.crc32(name.encode()), seed]).standard_normal(out[name].shape)
        drawn = base * np.exp(spread * noise) if base else spread * noise
        out[name] = jnp.asarray(drawn.astype(out[name].dtype))
    for name, factor in factors.items():
        out[name] = (out[name] * factor).astype(out[name].dtype)
    return out
```

```python
import concourse.bass as bass
from concourse import mybir
from contextlib import ExitStack

F32 = mybir.dt.float32
BF16 = mybir.dt.bfloat16
I32 = mybir.dt.int32
ALU = mybir.AluOpType
ACT = mybir.ActivationFunctionType
AX = mybir.AxisListType

P = 128
B, T, C = 2, 1024, 256
NTOK = B * T
NH, NG, D = 16, 4, 16
HG = NH // NG
NU = B * NG
E, H, I = 8, 256, 512
KC = C // P
NT = NTOK // P
CH = 512
NCH = NTOK // CH
TPC = CH // P
FC = I // P
NQ = T // P
M_ROWS, AL_ROWS = 3, 4
ROW0 = M_ROWS + AL_ROWS
Q_PART = (0, 0, 0, 1, 1, 2)
K_PART = (0, 1, 2, 0, 1, 0)
K_RUNS = ((0, 3), (3, 2), (5, 1))
KROWS = ROW0 + D * len(Q_PART)
SCALE = float(D) ** -0.5
EPS = 1e-5
MT = NTOK // P + E - 1
VW = D + 1
VP = 32
STEP = 3
LOOPS = (NU - 2) // STEP
assert LOOPS * STEP == NU - 2

CF_ID, CF_SEL, CF_IOTA, CF_THR, CF_LE, CF_J = 0, 128, 256, 264, 392, 456
CF_N = CF_J + MT * E
CB_ID, CB_MQK, CB_MKQ, CB_TRI, CB_ONE = 0, 128, 256, 768, 896
CB_N = 1024


def row_max_tiles():
    tiles = []
    for qi in range(NQ):
        w = min(qi + 1, 4) * P
        heads = [[0, 1, 2, 3]] if qi == 0 else [[0, 1], [2], [3]] if qi == 1 else [[h] for h in range(HG)]
        tiles += [(qi, hs[0], len(hs), 0, w, False) for hs in heads]
        if qi >= 4:
            w = (qi - 3) * P
            per = max(1, 4 * P // w) if w != 3 * P else 1
            tiles += [(qi, h, per, 4 * P, w, True) for h in range(0, HG, per)]
    return tiles


def prob_group(s):
    return [(j, 0, j, s) if s <= j else (j, 1, NQ - 1 - j, s - j - 1) for j in range(4)]


def first_tiles(n):
    lots = 3 * NCH - FIRST_A
    i = n - FIRST_A
    return range(i * (NA - 1) // lots, (i + 1) * (NA - 1) // lots)


FIRST_A = 9
A_TILES = row_max_tiles()
NA = len(A_TILES) + 1
GROUPS = 9
assert NA % 2 == 0 and GROUPS % STEP == 0


def layer(nc, x_d, xT_d, wq_d, wk_d, wv_d, wo_d, rt_d, gu_d, dn_d, sg_d, su_d, sd_d, cf_d, cb_d, al_d, one_d, zero_d,
          out_d):
    with ExitStack() as ctx:
        def sb(name, shape, dt=F32):
            return ctx.enter_context(nc.sbuf_tensor(name, shape, dt))

        def sem(name):
            return ctx.enter_context(nc.semaphore(name))

        qparts_d = nc.dram_tensor("qparts", [3, NU * HG * D, T], BF16, kind="Internal").ap()
        kparts_d = nc.dram_tensor("kparts", [3, NU * D, T], BF16, kind="Internal").ap()
        yT_d = nc.dram_tensor("yT", [NU * HG * D, T], F32, kind="Internal").ap()
        den_d = nc.dram_tensor("den", [NU * HG, T], F32, kind="Internal").ap()
        rden_d = nc.dram_tensor("rden", [NU * HG, T], F32, kind="Internal").ap()
        xs_d = nc.dram_tensor("xs", [MT * P, C], F32, kind="Internal").ap()
        ys_d = nc.dram_tensor("ys", [MT * P, C], F32, kind="Internal").ap()

        ps = ctx.enter_context(nc.psum_tensor("ps", [P, 8, 512], F32))

        wgu = sb("wgu", [P, E * KC * 2 * I])
        qk_or_dn = sb("qk_or_dn", [P, E * FC * H])
        qk16 = qk_or_dn[:, :].bitcast(BF16)
        Q6 = [qk16[:, i * HG * T:(i + 1) * HG * T].rearrange("p (h t) -> p h t", h=HG) for i in range(STEP)]
        k_at = STEP * HG * T
        K6 = [qk16[:, k_at + i * T:k_at + (i + 1) * T] for i in range(STEP)]
        wdn = qk_or_dn
        wsg = sb("wsg", [P, KC, I])
        wsu = sb("wsu", [P, KC, I])
        wsd = sb("wsd", [P, FC, H])
        x_all = sb("x_all", [P, NT, C])
        probs = sb("probs", [P, 3 * 4, 512])
        pr2 = probs[:, :, :].rearrange("p a b -> p (a b)")
        xTc = pr2[:, 0:NCH * KC * CH].rearrange("p (c k t) -> p c k t", c=NCH, k=KC)
        x1T = pr2[:, 0:KC * NTOK].rearrange("p (k t) -> p k t", k=KC)
        rows = sb("rows", [P, NT, C])
        V_all = sb("V_all", [P, NU, NQ, VW])
        Vs = sb("Vs", [P, STEP, NQ, VP])
        yU = sb("yU", [P, 2, 512])
        wq = yU[:, 0, :].rearrange("p (k n) -> p k n", k=KC)
        wkv = yU[:, 1, 0:KC * P].rearrange("p (k n) -> p k n", k=KC)
        wo = sb("wo", [P, KC, C])
        rt = sb("rt", [P, KC, E])
        cf = sb("cf", [P, CF_N])
        cb = sb("cb", [P, CB_N], BF16)
        tmp = sb("tmp", [P, 4608])
        t16 = tmp[:, 0:3 * 3 * CH // 2].bitcast(BF16)
        parts0 = [t16[:, r * 3 * CH:(r + 1) * 3 * CH].rearrange("p (a t) -> p a t", a=3) for r in range(3)]
        vT = tmp[NG * D:P, 3840:3840 + CH]
        rest0 = [tmp[:, 2304 + r * CH:2304 + (r + 1) * CH] for r in range(3)]
        yTc = [tmp[:, i * 1024:(i + 1) * 1024].rearrange("p (k t) -> p k t", k=KC) for i in range(2)]
        rdc = [tmp[0:8, 2048 + i * 1024:2048 + (i + 1) * 1024].rearrange("p (k t) -> p k t", k=KC) for i in range(2)]
        den = tmp[:, 4096:4096 + 256]
        hT = tmp[:, 0:2048].rearrange("p (f t) -> p f t", f=FC)
        sG = [tmp[:, 2048 + i * 512:2048 + (i + 1) * 512] for i in range(2)]
        esG = [tmp[:, i * 512:(i + 1) * 512] for i in range(2)]
        eh = [tmp[:, 1024 + i * 512:1024 + (i + 1) * 512] for i in range(2)]
        ehT = [tmp[:, 2048 + i * 512:2048 + (i + 1) * 512].rearrange("p (f t) -> p f t", f=FC) for i in range(2)]
        xs = [tmp[:, 3072 + i * 256:3072 + (i + 1) * 256] for i in range(2)]
        xsT = [tmp[:, 3584 + i * 256:3584 + (i + 1) * 256].rearrange("p (k t) -> p k t", k=KC) for i in range(2)]
        ys = [tmp[:, 4096 + i * 256:4096 + (i + 1) * 256] for i in range(2)]

        mx0 = sb("mx0", [P, HG, NQ])
        mx1 = sb("mx1", [P, HG, 4])
        mrest = sb("mrest", [P, HG * NQ])
        mparts = sb("mparts", [P, 3, HG * NQ], BF16)
        mrow = sb("mrow", [3 * HG * NQ, P], BF16)
        credit = sb("credit", [1, 8])
        bst = sb("bst", [P, NT, 6])
        mv = sb("mv", [P, NT, 2])
        rstd = sb("rstd", [P, NT])
        half = sb("half", [P, NT])
        lg = sb("lg", [P, NT, E])
        top = sb("top", [P, NT])
        eq = sb("eq", [P, NT, E])
        first = sb("first", [P, NT])
        oh = sb("oh", [P, NT, E])
        oh16 = sb("oh16", [P, NT, E], BF16)
        score = sb("score", [P, NT])
        many = sb("many", [P, E, NT])
        cnt = sb("cnt", [P, E])
        cum = sb("cum", [P, E, E])
        end = sb("end", [P, E])
        start = sb("start", [P, E])
        place = sb("place", [P, NT, E])
        slotf = sb("slotf", [P, NT])
        slot = sb("slot", [P, NT], I32)
        after = sb("after", [P, MT, E])
        etf = sb("etf", [P, MT])
        et = sb("et", [P, MT], I32)

        idf = cf[:, CF_ID:CF_ID + P]
        sel = cf[0:8, CF_SEL:CF_SEL + P]
        id16 = cb[:, CB_ID:CB_ID + P]
        mask_qk = cb[:, CB_MQK:CB_MQK + P]
        mask_kq = cb[:, CB_MKQ:CB_MKQ + HG * P]
        tri = cb[:, CB_TRI:CB_TRI + P]
        ones = cb[:, CB_ONE:CB_ONE + P]

        s_w0, s_x, s_wo, s_wsh, s_wgu, s_wdn = (sem(n) for n in ("s_w0", "s_x", "s_wo", "s_wsh", "s_wgu", "s_wdn"))
        s_xT = [sem(f"s_xT{i}") for i in range(NCH)]
        s_prj, s_ph, s_pr, s_pm, s_pl, s_vT, s_vps, s_vev = (
            sem(n) for n in ("s_prj", "s_ph", "s_pr", "s_pm", "s_pl", "s_vT", "s_vps", "s_vev"))
        s_pw = [sem(f"s_pw{i}") for i in range(3)]
        s_one, s_seen = sem("s_one"), sem("s_seen")
        s_qk = [sem(f"s_qk{i}") for i in range(STEP)]
        s_vinit, s_vs = sem("s_vinit"), sem("s_vs")
        s_aps, s_amax, s_split, s_mparts, s_mrow = (
            sem(n) for n in ("s_aps", "s_amax", "s_split", "s_mparts", "s_mrow"))
        s_st, s_exp, s_pv, s_yev = (sem(n) for n in ("s_st", "s_exp", "s_pv", "s_yev"))
        s_yst = [sem(f"s_yst{i}") for i in range(2)]
        s_den, s_rd, s_rds = sem("s_den"), sem("s_rd"), sem("s_rds")
        s_ch = [sem(f"s_ch{i}") for i in range(2)]
        s_rb, s_yn, s_op, s_res, s_bn, s_rstd, s_x1, s_tp, s_x1T, s_lg = (
            sem(n) for n in ("s_rb", "s_yn", "s_op", "s_res", "s_bn", "s_rstd", "s_x1", "s_tp", "s_x1T", "s_lg"))
        s_half = sem("s_half")
        s_zero, s_zf = sem("s_zero"), sem("s_zf")
        s_rt, s_oh, s_rank, s_ez, s_score, s_slot, s_xsc = (
            sem(n) for n in ("s_rt", "s_oh", "s_rank", "s_ez", "s_score", "s_slot", "s_xsc"))
        s_sc = sem("s_sc")
        s_g, s_u, s_sg, s_h, s_dn, s_acc = (sem(n) for n in ("s_g", "s_u", "s_sg", "s_h", "s_dn", "s_acc"))
        s_xs = [sem(f"s_xs{i}") for i in range(2)]
        s_et, s_ete, s_eg, s_eu, s_es, s_eh, s_eht, s_ehe, s_ed, s_ey = (
            sem(n) for n in ("s_et", "s_ete", "s_eg", "s_eu", "s_es", "s_eh", "s_eht", "s_ehe", "s_ed", "s_ey"))
        s_ys = [sem(f"s_ys{i}") for i in range(2)]
        s_gt = [sem(f"s_gt{i}") for i in range(NCH)]
        s_bn2, s_rstd2, s_fin, s_out = sem("s_bn2"), sem("s_rstd2"), sem("s_fin"), sem("s_out")

        NJ = 3 * NCH
        S_QK = 16 * (2 + len(Q_PART) + len(K_RUNS))

        block = ctx.enter_context(nc.Block())

        @block.sync
        def _(sp):
            def wait_for(sem, value):
                sp.wait_ge(sem, value)
                sp.sem_inc(s_seen, 1)

            def load_unit(u, i):
                sp.dma_start(Q6[i][0:M_ROWS, :, :].rearrange("p h t -> p (h t)"), zero_d).then_inc(s_qk[i], 16)
                sp.dma_start(K6[i][M_ROWS:ROW0, :], al_d[bass.ds(u * AL_ROWS, AL_ROWS), :]).then_inc(s_qk[i], 16)
                for s, part in enumerate(Q_PART):
                    r = ROW0 + s * D
                    sp.dma_start(Q6[i][r:r + D, :, :], qparts_d[part, bass.ds(u * HG * D, HG * D), :]
                                 .rearrange("(h d) t -> d h t", h=HG)).then_inc(s_qk[i], 16)
                for s, n in K_RUNS:
                    r = ROW0 + s * D
                    sp.dma_start(K6[i][r:r + n * D, :], kparts_d[0:n, bass.ds(u * D, D), :]).then_inc(s_qk[i], 16)

            def store_y(u, bank):
                wait_for(s_yev, u * 2 + (bank + 1 + 2))
                for j in range(4):
                    qi = j if bank == 0 else NQ - 1 - j
                    src = yU[32 * j:32 * j + VW, bank, :].rearrange("p (h t) -> p h t", h=HG)
                    sp.dma_start(yT_d[bass.ds(u * HG * D, HG * D), qi * P:(qi + 1) * P]
                                 .rearrange("(h d) t -> d h t", h=HG), src[0:D]).then_inc(s_yst[bank], 16)
                    sp.dma_start(den_d[bass.ds(u * HG, HG), qi * P:(qi + 1) * P]
                                 .rearrange("(o h) t -> o h t", o=1), src[D:VW]).then_inc(s_yst[bank], 16)

            def max_rows(u, i):
                sp.wait_ge(s_amax, u * NA + NA)
                n = HG * NQ
                for p in range(3):
                    sp.dma_start(Q6[i][p:p + 1, :, :].rearrange("o h t -> o (h t)")
                                 .rearrange("o (a b) -> o a b", a=n),
                                 mrow[p * n:(p + 1) * n, :]).then_inc(s_mrow, 16)

            def load_den(b):
                sp.dma_start(den[:, b * P:(b + 1) * P], den_d[b * NH:(b + 1) * NH, :]
                             .rearrange("a (b t) -> (a b) t", t=P)).then_inc(s_den, 16)

            def store_rden(b):
                sp.wait_ge(s_rd, b + 1)
                sp.dma_start(rden_d[b * NH:(b + 1) * NH, :].rearrange("a (b t) -> (a b) t", t=P),
                             den[:, b * P:(b + 1) * P]).then_inc(s_rds, 16)
                sp.wait_ge(s_rds, 16 * (b + 1))

            def load_yT(c):
                b, col = c // 2, (c % 2) * CH
                sp.dma_start(yTc[c % 2], yT_d[b * C:(b + 1) * C, col:col + CH]
                             .rearrange("(k p) t -> p k t", p=P)).then_inc(s_ch[c % 2], 16)

            def load_rden(c):
                b, col = c // 2, (c % 2) * CH
                sp.dma_start(rdc[c % 2], rden_d[b * NH:(b + 1) * NH, col:col + CH]
                             .rearrange("(k p) t -> p k t", p=8)).then_inc(s_ch[c % 2], 16)

            def step(u, k, last=False, more=True):
                if more:
                    sp.wait_ge(s_pv, u * GROUPS + 3)
                    load_unit(u + 2, (k + 2) % STEP)
                store_y(u, 0)
                if not last:
                    max_rows(u + 1, (k + 1) % STEP)
                store_y(u, 1)

            def load_x(c):
                sp.dma_start(xTc[:, c], xT_d[:, c * CH:(c + 1) * CH].rearrange("(k p) t -> p k t", p=P)
                             ).then_inc(s_xT[c], 16)

            load_x(0)
            sp.dma_start(wq, wq_d.rearrange("(k p) n -> p k n", p=P)).then_inc(s_w0, 16)
            sp.dma_start(wkv[:, :, 0:NG * D], wk_d.rearrange("(k p) n -> p k n", p=P)).then_inc(s_w0, 16)
            sp.dma_start(wkv[:, :, NG * D:P], wv_d.rearrange("(k p) n -> p k n", p=P)).then_inc(s_w0, 16)
            load_x(1)
            sp.dma_start(cf[:], cf_d).then_inc(s_w0, 16)
            sp.dma_start(cb[:], cb_d).then_inc(s_w0, 16)
            load_x(2)
            load_x(3)
            for i in range(STEP):
                sp.dma_start(Q6[i][M_ROWS:ROW0, :, :].rearrange("p h t -> p (h t)"), one_d).then_inc(s_one, 16)
                sp.dma_start(K6[i][0:M_ROWS, :], one_d[0:M_ROWS, 0:T]).then_inc(s_one, 16)
            for n in range(NJ):
                sp.wait_ge(s_pl, n + 1)
                c, k = n // 3, n % 3
                b, col = c // 2, (c % 2) * CH
                if k < 2:
                    r, m, dst = b * NH * D + k * P, P, qparts_d
                else:
                    r, m, dst = b * NG * D, NG * D, kparts_d
                sp.dma_start(dst[:, r:r + m, col:col + CH].rearrange("a r t -> r a t"),
                             parts0[n % 3][0:m, :, :]).then_inc(s_pw[n % 3], 16)
                if n == NJ // 2 - 1:
                    for i in range(3):
                        sp.wait_ge(s_pw[i], 16 * NJ // 6)
                    for u in range(2):
                        load_unit(u, u)
            for i in range(3):
                sp.wait_ge(s_pw[i], 16 * NJ // 3)
            max_rows(0, 0)
            with sp.Fori(0, LOOPS, 1) as it:
                for k in range(STEP):
                    step(it * STEP + k, k)
            for u in range(LOOPS * STEP, NU):
                step(u, u % STEP, last=(u == NU - 1), more=False)
                if u == NU - 2:
                    load_den(0)
                    store_rden(0)
                    for c in range(2):
                        load_yT(c)
                        load_rden(c)

            for i in range(2):
                sp.wait_ge(s_yst[i], 128 * (NU + 1))
            load_den(1)
            for e in range(E):
                sp.dma_start(wdn[:, e * FC * H:(e + 1) * FC * H].rearrange("p (f n) -> p f n", f=FC),
                             dn_d[e].rearrange("(f p) n -> p f n", p=P)).then_inc(s_wdn, 16)
            for c in range(2, NCH):
                sp.wait_ge(s_op, TPC * (c - 1))
                load_yT(c)
                if c == 2:
                    store_rden(1)
                load_rden(c)

            def load_tile(j, k):
                sp.dma_start(xs[k], xs_d[bass.ds(j * P, P), :]).then_inc(s_xs[k], 16)

            def store_tile(j, k):
                wait_for(s_ey, j + 1)
                sp.dma_start(ys_d[bass.ds(j * P, P), :], ys[k]).then_inc(s_ys[k], 16)

            sp.wait_ge(s_sc, 16 * NT)
            sp.wait_ge(s_acc, NT)
            load_tile(0, 0)
            load_tile(1, 1)

            def expert_step(j, k):
                wait_for(s_et, j + 1)
                load_tile(j + 2, k)
                store_tile(j, k)

            for j in range(2):
                expert_step(j, j)
            with sp.Fori(1, (MT - 3) // 2, 1) as it:
                for k in range(2):
                    expert_step(it * 2 + k, k)
            for j in range((MT - 3) // 2 * 2, MT):
                if j + 2 < MT:
                    expert_step(j, j % 2)
                else:
                    store_tile(j, j % 2)

            out_t = out_d.rearrange("(n p) c -> p n c", p=P)
            for c in range(NCH):
                sp.wait_ge(s_fin, c + 1)
                sp.dma_start(out_t[:, c * TPC:(c + 1) * TPC, :], x_all[:, c * TPC:(c + 1) * TPC, :]).then_inc(s_out, 16)
            sp.wait_ge(s_out, 16 * NCH)
            for i in range(2):
                sp.wait_ge(s_ys[i], 16 * ((MT + 1 - i) // 2))

        @block.tensor
        def _(pe):
            pe.wait_ge(s_w0, 16 * 5)
            def job(n):
                c, k = n // 3, n % 3
                pe.wait_ge(s_xT[c], 16)
                if n >= 4:
                    pe.wait_ge(s_pr, n - 3)
                if n >= 6 and (n - 4) % 3 == 2:
                    pe.wait_ge(s_vT, (n - 4) // 3 + 1)
                for kc in range(KC):
                    w = wq[:, kc, k * P:(k + 1) * P] if k < 2 else wkv[:, kc, :]
                    mm = pe.matmul(ps[:, 4 + n % 4, :], w, xTc[:, c, kc, :], start=kc == 0, stop=kc == KC - 1)
                mm.then_inc(s_prj, 1)

            def values(c):
                pe.wait_ge(s_vT, c + 1)
                if c >= 2:
                    pe.wait_ge(s_vev, c - 1)
                for t in range(TPC):
                    mm = pe.transpose(ps[:, 2 + c % 2, t * NG * D:(t + 1) * NG * D], vT[:, t * P:(t + 1) * P],
                                      cf[NG * D:P, CF_ID + NG * D:CF_ID + P])
                mm.then_inc(s_vps, 1)

            def max_tile(u, k, t):
                bank = t % 2
                if isinstance(u, int) and u == 0:
                    if t >= 2:
                        pe.wait_ge(s_amax, t - 1)
                else:
                    pe.wait_ge(s_amax, u * NA + t - 1)
                if t == NA - 1:
                    pe.wait_ge(s_mparts, u + 1)
                    pe.transpose(ps[0:3 * HG * NQ, bank, 0:P // 2].bitcast(BF16),
                                 mparts[:, :, :].rearrange("p a b -> p (a b)"), id16).then_inc(s_aps, 1)
                    return
                qi, h0, nh, k0, w, _ = A_TILES[t]
                diag = qi * P - k0
                for i in range(nh):
                    q = Q6[k][0:KROWS, h0 + i, qi * P:(qi + 1) * P]
                    o = ps[:, bank, i * w:(i + 1) * w]
                    masked = diag < w
                    mm = pe.matmul(o, q, K6[k][0:KROWS, k0:k0 + w], start=True, stop=not masked)
                    if masked:
                        mm = pe.matmul(o[:, diag:diag + P], id16, mask_qk, start=False, stop=True)
                mm.then_inc(s_aps, 1)

            def scores(u, k, s):
                for j, bank, qi, kb in prob_group(s):
                    if j % 2 == 0:
                        pe.wait_ge(s_exp, u * (2 * GROUPS) + 2 * s + j // 2 + 1)
                    o = ps[:, 4 + j, :]
                    if kb == qi:
                        pe.matmul(o, id16, mask_kq, start=True, stop=False)
                    mm = pe.matmul(o, K6[k][0:KROWS, kb * P:(kb + 1) * P],
                                   Q6[k][0:KROWS, :, qi * P:(qi + 1) * P], start=kb != qi, stop=True)
                    if j % 2 == 1:
                        mm.then_inc(s_st, 1)

            def weigh(u, k, s):
                pe.wait_ge(s_exp, u * (2 * GROUPS) + 2 * s + 4)
                if s <= 1:
                    pe.wait_ge(s_yev, u * 2 + s + 1)
                for j, bank, qi, kb in prob_group(s):
                    mm = pe.matmul(ps[32 * j:32 * j + VP, 2 + bank, :], Vs[:, k, kb, :], probs[:, 4 * (s % 3) + j, :],
                                   start=kb == 0, stop=kb == qi, skip_group_check=True)
                mm.then_inc(s_pv, 1)

            def step(u, k, last=False):
                todo = [] if last else list(range(NA))
                if not last:
                    pe.wait_ge(s_qk[(k + 1) % STEP], S_QK * NEXT(u, k))

                def some(n):
                    n = max(n, 0)
                    for t in todo[:n]:
                        max_tile(u + 1, (k + 1) % STEP, t)
                    del todo[:n]

                some(4)
                pe.wait_ge(s_mrow, u * 48 + 48)
                pe.wait_ge(s_vs, u + 1)
                for s in range(GROUPS):
                    scores(u, k, s)
                    some(min(3, len(todo) - 1) if s < GROUPS - 1 else 1)
                    if s:
                        weigh(u, k, s - 1)
                    if s < GROUPS - 1:
                        some(min(2, len(todo) - 1))
                weigh(u, k, GROUPS - 1)

            def NEXT(u, k):
                if isinstance(u, int):
                    return (u + 1) // STEP + 1
                return IT[0] + (2 if k == STEP - 1 else 1)

            IT = [None]
            for n in range(NJ):
                job(n)
                if n % 3 == 0 and n:
                    values(n // 3 - 1)
                if n == FIRST_A:
                    pe.wait_ge(s_one, 32 * STEP)
                    pe.wait_ge(s_qk[0], S_QK)
                if n >= FIRST_A:
                    for t in first_tiles(n):
                        max_tile(0, 0, t)
            values(NCH - 1)
            max_tile(0, 0, NA - 1)
            with pe.Fori(0, LOOPS, 1) as it:
                IT[0] = it
                for k in range(STEP):
                    step(it * STEP + k, k)
            for u in range(LOOPS * STEP, NU):
                step(u, u % STEP, last=u == NU - 1)

            def project(c):
                pe.wait_ge(s_ch[c % 2], 32 * (c // 2 + 1))
                if c >= 1:
                    pe.wait_ge(s_yn, c)
                for kc in range(KC):
                    mm = pe.matmul(ps[:, kc, :], sel, rdc[c % 2][:, kc, :], start=True, stop=True)
                mm.then_inc(s_rb, 1)
                pe.wait_ge(s_yn, c + 1)
                for t in range(TPC):
                    n = c * TPC + t
                    if n >= 2:
                        pe.wait_ge(s_res, n - 1)
                    for kc in range(KC):
                        mm = pe.matmul(ps[:, 2 + n % 2, 0:C], yTc[c % 2][:, kc, t * P:(t + 1) * P], wo[:, kc, :],
                                       start=kc == 0, stop=kc == KC - 1)
                    mm.then_inc(s_op, 1)

            def route(c):
                pe.wait_ge(s_x1, c + 1)
                if c >= 1:
                    pe.wait_ge(s_x1T, KC * c)
                for kc in range(KC):
                    for t in range(TPC):
                        mm = pe.transpose(ps[:, 4 + kc, t * P:(t + 1) * P],
                                          x_all[:, c * TPC + t, kc * P:(kc + 1) * P], idf)
                    mm.then_inc(s_tp, 1)
                pe.wait_ge(s_x1T, KC * (c + 1))
                for t in range(TPC):
                    n = c * TPC + t
                    for kc in range(KC):
                        mm = pe.matmul(ps[:, 6, n * E:(n + 1) * E], x1T[:, kc, n * P:(n + 1) * P], rt[:, kc, :],
                                       start=kc == 0, stop=kc == KC - 1)
                mm.then_inc(s_lg, 1)

            pe.wait_ge(s_wo, 32)
            pe.wait_ge(s_yev, 2 * NU + 2)
            project(0)
            for c in range(NCH):
                if c + 1 < NCH:
                    project(c + 1)
                route(c)

            def gate_up(n):
                c, f = n // FC, n % FC
                if n >= 2:
                    pe.wait_ge(s_h, n - 1)
                for w, bank, done in ((wsg, 0, s_g), (wsu, 1, s_u)):
                    for kc in range(KC):
                        mm = pe.matmul(ps[:, bank + 2 * (n % 2), :], w[:, kc, f * P:(f + 1) * P],
                                       x1T[:, kc, c * CH:(c + 1) * CH], start=kc == 0, stop=kc == KC - 1)
                    mm.then_inc(done, 1)

            def down(c):
                pe.wait_ge(s_h, FC * (c + 1))
                for t in range(TPC):
                    n = c * TPC + t
                    if n >= 2:
                        pe.wait_ge(s_acc, n - 1)
                    for f in range(FC):
                        mm = pe.matmul(ps[:, 4 + n % 2, 0:H], hT[:, f, t * P:(t + 1) * P], wsd[:, f, :],
                                       start=f == 0, stop=f == FC - 1)
                    mm.then_inc(s_dn, 1)

            pe.wait_ge(s_wsh, 48)
            pe.wait_ge(s_res, NT)
            gate_up(0)
            gate_up(1)
            pe.wait_ge(s_oh, 1)
            flat = oh16[:, :, :].rearrange("p n e -> p (n e)")
            pe.matmul(ps[:, 7, 0:NT * E], tri, flat, start=True, stop=False, skip_group_check=True)
            for n in range(NT - 1):
                later = ps[:, 7, (n + 1) * E:NT * E].rearrange("p (n e) -> p n e", e=E)
                pe.matmul(later, ones, oh16[:, n:n + 1, :].broadcast_to([P, NT - 1 - n, E]), start=False,
                          stop=n == NT - 2, skip_group_check=True)
            for n in range(NT):
                mm = pe.matmul(ps[:, 6, 256:256 + E], ones, oh16[:, n, :], start=n == 0, stop=n == NT - 1)
            mm.then_inc(s_rank, 1)
            gate_up(2)
            gate_up(3)
            for c in range(NCH):
                if c + 1 < NCH:
                    gate_up(FC * (c + 1))
                    gate_up(FC * (c + 1) + 1)
                down(c)
                if c + 1 < NCH:
                    gate_up(FC * (c + 1) + 2)
                    gate_up(FC * (c + 1) + 3)

            def expert_up(j, k, peeled=None):
                pe.wait_ge(s_xs[k], (peeled // 2 + 1) * 16 if peeled is not None else (IT[0] * 16 + (16 if k else 32)))
                if peeled is None or peeled >= 1:
                    pe.wait_ge(s_ete, j)
                for kc in range(KC):
                    mm = pe.transpose(ps[:, 6, kc * P:(kc + 1) * P], xs[k][:, kc * P:(kc + 1) * P], idf)
                mm.then_inc(s_et, 1)
                e = pe.value_load(et[0:1, bass.ds(j, 1)], min_val=0, max_val=E - 1)
                pe.wait_ge(s_ete, j + 1)
                if peeled is None or peeled >= 2:
                    pe.wait_ge(s_eh, j - 1)
                for half_i, done in ((0, s_eg), (1, s_eu)):
                    for kc in range(KC):
                        mm = pe.matmul(ps[:, 2 * k + half_i, :], xsT[k][:, kc, :],
                                       wgu[:, bass.ds(e * (KC * 2 * I) + (kc * 2 * I + half_i * I), I)],
                                       start=kc == 0, stop=kc == KC - 1)
                    mm.then_inc(done, 1)

            def expert_down(j, k, peeled=None):
                e = pe.value_load(et[0:1, bass.ds(j, 1)], min_val=0, max_val=E - 1)
                pe.wait_ge(s_eh, j + 1)
                if peeled is None or peeled >= 2:
                    pe.wait_ge(s_ehe, j - 1)
                for f in range(FC):
                    mm = pe.transpose(ps[:, 4 + k, f * P:(f + 1) * P], eh[k][:, f * P:(f + 1) * P], idf)
                mm.then_inc(s_eht, 1)
                pe.wait_ge(s_ehe, j + 1)
                if peeled is None or peeled >= 1:
                    pe.wait_ge(s_ey, j)
                for f in range(FC):
                    mm = pe.matmul(ps[:, 7, 0:H], ehT[k][:, f, :], wdn[:, bass.ds(e * (FC * H) + f * H, H)],
                                   start=f == 0, stop=f == FC - 1)
                mm.then_inc(s_ed, 1)

            pe.wait_ge(s_wgu, 16 * E)
            pe.wait_ge(s_wdn, 16 * E)
            pe.wait_ge(s_slot, 1)
            pe.wait_ge(s_acc, NT)
            expert_up(0, 0, peeled=0)
            for j in range(2):
                expert_up(j + 1, (j + 1) % 2, peeled=j + 1)
                expert_down(j, j, peeled=j)
            with pe.Fori(1, (MT - 1) // 2, 1) as it:
                IT[0] = it
                for k in range(2):
                    expert_up(it * 2 + (k + 1), 1 - k)
                    expert_down(it * 2 + k, k)
            expert_down(MT - 1, (MT - 1) % 2, peeled=MT - 1)

        @block.scalar
        def _(act):
            def put_values(c):
                act.wait_ge(s_vps, c + 1)
                b = c // 2
                for t in range(TPC):
                    kb = (c % 2) * TPC + t
                    ins = act.activation(V_all[:, b * NG:(b + 1) * NG, kb, 0:D],
                                         ps[:, 2 + c % 2, t * NG * D:(t + 1) * NG * D].rearrange("p (g d) -> p g d", g=NG),
                                         ACT.Copy)
                ins.then_inc(s_vev, 1)

            for n in range(NJ):
                c, k = n // 3, n % 3
                m = P if k < 2 else NG * D
                act.wait_ge(s_prj, n + 1)
                if n >= 3:
                    act.wait_ge(s_pw[n % 3], 16 * (n // 3))
                act.activation(parts0[n % 3][0:m, 0, :], ps[0:m, 4 + n % 4, :], ACT.Copy).then_inc(s_ph, 1)
                if k == 2:
                    if c >= 1:
                        act.wait_ge(s_vps, c)
                    act.activation(vT, ps[NG * D:P, 4 + n % 4, :], ACT.Copy).then_inc(s_vT, 1)
                if k == 0 and c:
                    put_values(c - 1)
            put_values(NCH - 1)
            for e in range(E):
                act.dma_start(wgu[:, e * KC * 2 * I:(e + 1) * KC * 2 * I].rearrange("p (k n) -> p k n", k=KC),
                             gu_d[e].rearrange("(k p) n -> p k n", p=P)).then_inc(s_wgu, 16)
            act.dma_start(wsg[:], sg_d.rearrange("(k p) n -> p k n", p=P)).then_inc(s_wsh, 16)
            act.dma_start(wsu[:], su_d.rearrange("(k p) n -> p k n", p=P)).then_inc(s_wsh, 16)
            act.dma_start(wsd[:], sd_d.rearrange("(k p) n -> p k n", p=P)).then_inc(s_wsh, 16)
            act.dma_start(x_all[:], x_d.rearrange("(n p) c -> p n c", p=P)).then_inc(s_x, 16)
            act.dma_start(wo[:], wo_d.rearrange("(k p) n -> p k n", p=P)).then_inc(s_wo, 16)
            act.dma_start(rt[:], rt_d.rearrange("(k p) n -> p k n", p=P)).then_inc(s_wo, 16)
            act.wait_ge(s_zero, 1)
            xs_t = xs_d.rearrange("(n p) c -> p n c", p=P)
            act.dma_start(xs_t[:, 0:NT, :], rows[:]).then_inc(s_zf, 16)
            act.dma_start(xs_t[:, NT:MT, :], rows[:, 0:MT - NT, :]).then_inc(s_zf, 16)

            def step(u, k):
                for s in range(GROUPS):
                    for hb in range(2):
                        act.wait_ge(s_st, u * (2 * GROUPS) + 2 * s + hb + 1)
                        if hb == 0:
                            act.wait_ge(s_pv, u * GROUPS + s + 1)
                        act.activation(probs[:, 4 * (s % 3) + 2 * hb:4 * (s % 3) + 2 * hb + 2, :],
                                       ps[:, 4 + 2 * hb:6 + 2 * hb, :], ACT.Exp, scale=SCALE).then_inc(s_exp, 1)
                    if s == 4:
                        act.wait_ge(s_pv, u * GROUPS + 4 + 3)
                        act.wait_ge(s_yst[0], u * 128 + 128)
                        act.activation(yU[:, 0, :], ps[:, 2, :], ACT.Copy).then_inc(s_yev, 1)
                act.wait_ge(s_pv, u * GROUPS + GROUPS + 3)
                act.wait_ge(s_yst[1], u * 128 + 128)
                act.activation(yU[:, 1, :], ps[:, 3, :], ACT.Copy).then_inc(s_yev, 1)

            with act.Fori(0, LOOPS, 1) as it:
                for k in range(STEP):
                    step(it * STEP + k, k)
            for u in range(LOOPS * STEP, NU):
                step(u, u % STEP)

            for c in range(NCH):
                for kc in range(KC):
                    act.wait_ge(s_tp, KC * c + kc + 1)
                    act.activation(x1T[:, kc, c * CH:(c + 1) * CH], ps[:, 4 + kc, :], ACT.Copy).then_inc(s_x1T, 1)
            act.wait_ge(s_rt, 2)
            act.activation(score[:], top[:], ACT.Exp, scale=-1.0).then_inc(s_ez, 1)
            for n in range(NCH * FC):
                act.wait_ge(s_g, n + 1)
                if n >= 2:
                    act.wait_ge(s_h, n - 1)
                act.activation(sG[n % 2], ps[:, 2 * (n % 2), :], ACT.Silu).then_inc(s_sg, 1)

            def expert_up(j, k, peeled=None):
                act.wait_ge(s_et, j + 1)
                if peeled is None or peeled >= 2:
                    act.wait_ge(s_eu, j - 1)
                act.activation(xsT[k].rearrange("p k t -> p (k t)"), ps[:, 6, 0:C], ACT.Copy).then_inc(s_ete, 1)
                act.wait_ge(s_eg, j + 1)
                if peeled is None or peeled >= 2:
                    act.wait_ge(s_eh, j - 1)
                act.activation(esG[k], ps[:, 2 * k, :], ACT.Silu).then_inc(s_es, 1)

            def expert_down(j, k, peeled=None):
                act.wait_ge(s_eht, j + 1)
                if peeled is None or peeled >= 2:
                    act.wait_ge(s_ed, j - 1)
                act.activation(ehT[k].rearrange("p f t -> p (f t)"), ps[:, 4 + k, :], ACT.Copy).then_inc(s_ehe, 1)

            expert_up(0, 0, peeled=0)
            for j in range(2):
                expert_up(j + 1, (j + 1) % 2, peeled=j + 1)
                expert_down(j, j, peeled=j)
            with act.Fori(1, (MT - 1) // 2, 1) as it:
                for k in range(2):
                    expert_up(it * 2 + (k + 1), 1 - k)
                    expert_down(it * 2 + k, k)
            expert_down(MT - 1, (MT - 1) % 2, peeled=MT - 1)

        @block.vector
        def _(dve):
            def reduce_tile(u, t):
                qi, h0, nh, k0, w, second = A_TILES[t]
                dve.wait_ge(s_aps, u * NA + t + 1)
                o = mx1[:, h0:h0 + nh, qi - 4] if second else mx0[:, h0:h0 + nh, qi]
                dve.tensor_reduce(o, ps[:, t % 2, 0:nh * w].rearrange("p (h w) -> p h w", h=nh), AX.X,
                                  ALU.max).then_inc(s_amax, 1)

            for n in range(NJ):
                m = P if n % 3 < 2 else NG * D
                h, md, rest = parts0[n % 3][0:m, 0, :], parts0[n % 3][0:m, 1, :], rest0[n % 3][0:m, :]
                dve.wait_ge(s_ph, n + 1)
                if n >= 3:
                    dve.wait_ge(s_pl, n - 2)
                dve.tensor_tensor(rest, ps[0:m, 4 + n % 4, :], h, ALU.subtract).then_inc(s_pr, 1)
                dve.wait_ge(s_pr, n + 1)
                dve.tensor_copy(md, rest).then_inc(s_pm, 1)
                if n >= FIRST_A:
                    for t in first_tiles(n):
                        reduce_tile(0, t)
            dve.wait_ge(s_vev, NCH)
            dve.memset(credit[:, 0:1], 0.0).then_inc(s_exp, 2)
            dve.memset(credit[:, 1:2], 0.0).then_inc(s_pv, 3)
            dve.memset(credit[:, 2:3], 0.0).then_inc(s_yev, 2)
            dve.memset(credit[:, 3:4], 0.0).then_inc(s_yst[0], 128)
            dve.memset(credit[:, 4:5], 0.0).then_inc(s_yst[1], 128)

            def row_max(u):
                first_unit = isinstance(u, int) and u == 0
                if not first_unit:
                    dve.wait_ge(s_mparts, u)
                    for t in range(NA - 1):
                        reduce_tile(u, t)
                dve.wait_ge(s_amax, u * NA + NA - 1)
                dve.tensor_tensor(mx0[:, :, 4:NQ], mx0[:, :, 4:NQ], mx1[:], ALU.max).then_inc(s_split, 1)
                dve.wait_ge(s_split, u * 4 + 1)
                m = mx0[:, :, :].rearrange("p h q -> p (h q)")
                dve.tensor_scalar(mparts[:, 0, :], m, -1.0, None, ALU.mult).then_inc(s_split, 1)
                dve.wait_ge(s_split, u * 4 + 2)
                dve.scalar_tensor_tensor(mrest[:], m, -1.0, mparts[:, 0, :], ALU.mult, ALU.subtract).then_inc(s_split, 1)
                dve.wait_ge(s_split, u * 4 + 3)
                dve.tensor_copy(mparts[:, 1, :], mrest[:]).then_inc(s_split, 1)
                dve.wait_ge(s_split, u * 4 + 4)
                dve.tensor_tensor(mparts[:, 2, :], mrest[:], mparts[:, 1, :], ALU.subtract).then_inc(s_mparts, 1)
                dve.wait_ge(s_aps, u * NA + NA)
                if not first_unit:
                    dve.wait_ge(s_mrow, u * 48)
                dve.tensor_copy(mrow[:], ps[0:3 * HG * NQ, (NA - 1) % 2, 0:P // 2].bitcast(BF16)).then_inc(s_amax, 1)

            row_max(0)
            with dve.Fori(0, LOOPS, 1) as it:
                for k in range(STEP):
                    row_max(it * STEP + (k + 1))
            for u in range(LOOPS * STEP, NU - 1):
                row_max(u + 1)

            def invert(b):
                dve.wait_ge(s_den, 16 * (b + 1))
                dve.reciprocal(den[:, b * P:(b + 1) * P], den[:, b * P:(b + 1) * P]).then_inc(s_rd, 1)

            invert(0)

            def normalise(c):
                dve.wait_ge(s_rb, c + 1)
                y = yTc[c % 2].rearrange("p k t -> p (k t)")
                dve.tensor_tensor(y, y, ps[:, 0:KC, :].rearrange("p k t -> p (k t)"), ALU.mult).then_inc(s_yn, 1)

            def residual(c):
                for n in range(c * TPC, (c + 1) * TPC):
                    dve.wait_ge(s_op, n + 1)
                    dve.tensor_tensor(x_all[:, n, :], ps[:, 2 + n % 2, 0:C], x_all[:, n, :], ALU.add).then_inc(s_res, 1)

            def stats(c, done, base):
                for n in range(c * TPC, (c + 1) * TPC):
                    dve.bn_stats(bst[:, n, :], x_all[:, n, :]).then_inc(done, 1)
                for i, n in enumerate(range(c * TPC, (c + 1) * TPC)):
                    dve.wait_ge(done, base + i + 1)
                    ins = dve.bn_aggr(mv[:, n, :], bst[:, n, :]).then_inc(done, 1)

            def scale_rows(c):
                for n in range(c * TPC, (c + 1) * TPC):
                    ins = dve.tensor_scalar(x_all[:, n, :], x_all[:, n, :], mv[:, n, 0:1], rstd[:, n:n + 1],
                                            ALU.subtract, ALU.mult)
                return ins

            dve.wait_ge(s_x, 16)
            normalise(0)
            invert(1)
            for c in range(NCH):
                residual(c)
                dve.wait_ge(s_res, TPC * (c + 1))
                stats(c, s_bn, 2 * TPC * c)
                if c + 1 < NCH:
                    normalise(c + 1)
                dve.wait_ge(s_rstd, c + 1)
                scale_rows(c).then_inc(s_x1, 1)

            count = [0]

            def chain(ins):
                count[0] += 1
                ins.then_inc(s_rt, 1)
                dve.wait_ge(s_rt, count[0])

            def over_e(ap):
                return ap.rearrange("p (n o) -> p n o", o=1).broadcast_to([P, NT, E])

            iota = cf[:, CF_IOTA:CF_IOTA + E].rearrange("p (o e) -> p o e", o=1).broadcast_to([P, NT, E])
            dve.wait_ge(s_lg, NCH)
            chain(dve.tensor_copy(lg[:, :, :].rearrange("p n e -> p (n e)"), ps[:, 6, 0:NT * E]))
            chain(dve.tensor_reduce(top[:], lg[:], AX.X, ALU.max))
            chain(dve.tensor_tensor(eq[:], lg[:], over_e(top[:]), ALU.is_equal))
            chain(dve.tensor_tensor(eq[:], eq[:], iota, ALU.mult))
            chain(dve.tensor_reduce(first[:], eq[:], AX.X, ALU.min))
            chain(dve.tensor_tensor(oh[:], iota, over_e(first[:]), ALU.is_equal))
            dve.tensor_copy(oh16[:], oh[:]).then_inc(s_oh, 1)
            dve.wait_ge(s_ez, 1)
            chain(dve.tensor_scalar(score[:], score[:], 1.0, None, ALU.add))
            dve.reciprocal(score[:], score[:]).then_inc(s_score, 1)
            dve.wait_ge(s_rank, 1)
            chain(dve.tensor_copy(cnt[:], ps[:, 6, 256:256 + E]))
            chain(dve.tensor_tensor(many[:], cnt[:, :].rearrange("p (e o) -> p e o", o=1).broadcast_to([P, E, NT]),
                                    cf[:, CF_THR:CF_THR + E * NT].rearrange("p (e n) -> p e n", e=E), ALU.is_gt))
            chain(dve.tensor_reduce(cnt[:], many[:], AX.X, ALU.add))
            chain(dve.tensor_tensor(cum[:], cnt[:, :].rearrange("p (o e) -> p o e", o=1).broadcast_to([P, E, E]),
                                    cf[:, CF_LE:CF_LE + E * E].rearrange("p (a b) -> p a b", a=E), ALU.mult))
            chain(dve.tensor_reduce(end[:], cum[:], AX.X, ALU.add))
            chain(dve.tensor_tensor(start[:], end[:], cnt[:], ALU.subtract))
            chain(dve.tensor_scalar(start[:], start[:], float(P), None, ALU.mult))
            chain(dve.tensor_tensor(place[:], ps[:, 7, 0:NT * E].rearrange("p (n e) -> p n e", e=E),
                                    start[:, :].rearrange("p (o e) -> p o e", o=1).broadcast_to([P, NT, E]), ALU.add))
            chain(dve.tensor_tensor(place[:], place[:], oh[:], ALU.mult))
            chain(dve.tensor_reduce(slotf[:], place[:], AX.X, ALU.add))
            chain(dve.tensor_copy(slot[:], slotf[:]))
            chain(dve.tensor_tensor(after[:], cf[:, CF_J:CF_J + MT * E].rearrange("p (j e) -> p j e", e=E),
                                    end[:, :].rearrange("p (o e) -> p o e", o=1).broadcast_to([P, MT, E]), ALU.is_ge))
            chain(dve.tensor_reduce(etf[:], after[:], AX.X, ALU.add))
            chain(dve.tensor_scalar(etf[:], etf[:], float(E - 1), None, ALU.min))
            dve.tensor_copy(et[:], etf[:]).then_inc(s_slot, 1)

            def hidden(n):
                c, f = n // FC, n % FC
                dve.wait_ge(s_sg, n + 1)
                dve.wait_ge(s_u, n + 1)
                if f == 0 and c >= 1:
                    dve.wait_ge(s_dn, TPC * c)
                dve.tensor_tensor(hT[:, f, :], sG[n % 2], ps[:, 2 * (n % 2) + 1, :], ALU.mult).then_inc(s_h, 1)

            for n in range(FC):
                hidden(n)
            for c in range(NCH):
                for n in range(c * TPC, (c + 1) * TPC):
                    dve.wait_ge(s_dn, n + 1)
                    dve.wait_ge(s_xsc, n + 1)
                    dve.tensor_tensor(x_all[:, n, :], ps[:, 4 + n % 2, 0:H], x_all[:, n, :], ALU.add).then_inc(s_acc, 1)
                if c + 1 < NCH:
                    for n in range(FC):
                        hidden(FC * (c + 1) + n)

            def expert_up(j, k, peeled=None):
                dve.wait_ge(s_es, j + 1)
                dve.wait_ge(s_eu, j + 1)
                if peeled is None or peeled >= 2:
                    dve.wait_ge(s_eht, j - 1)
                dve.tensor_tensor(eh[k], esG[k], ps[:, 2 * k + 1, :], ALU.mult).then_inc(s_eh, 1)

            def expert_down(j, k, peeled=None):
                dve.wait_ge(s_ed, j + 1)
                if peeled is None:
                    dve.wait_ge(s_ys[k], IT[0] * 16)
                elif peeled >= 2:
                    dve.wait_ge(s_ys[k], peeled // 2 * 16)
                dve.tensor_copy(ys[k], ps[:, 7, 0:H]).then_inc(s_ey, 1)

            IT = [None]
            expert_up(0, 0, peeled=0)
            for j in range(2):
                expert_up(j + 1, (j + 1) % 2, peeled=j + 1)
                expert_down(j, j, peeled=j)
            with dve.Fori(1, (MT - 1) // 2, 1) as it:
                IT[0] = it
                for k in range(2):
                    expert_up(it * 2 + (k + 1), 1 - k)
                    expert_down(it * 2 + k, k)
            expert_down(MT - 1, (MT - 1) % 2, peeled=MT - 1)

            for c in range(NCH):
                dve.wait_ge(s_gt[c], 16 * TPC)
                if c == 0:
                    dve.wait_ge(s_acc, NT)
                v = slice(c * TPC, (c + 1) * TPC)
                dve.tensor_tensor(x_all[:, v, :], x_all[:, v, :], rows[:, v, :], ALU.add).then_inc(s_bn2, 1)
                base = (2 * TPC + 1) * c + 1
                dve.wait_ge(s_bn2, base)
                stats(c, s_bn2, base)
                dve.wait_ge(s_rstd2, c + 1)
                scale_rows(c).then_inc(s_fin, 1)

        @block.gpsimd
        def _(pool):
            pool.memset(V_all[:, :, :, D:VW], 1.0).then_inc(s_vinit, 1)
            pool.memset(Vs[:], 0.0).then_inc(s_vinit, 1)
            pool.memset(rows[:], 0.0).then_inc(s_zero, 1)
            pool.memset(half[:], -0.5).then_inc(s_half, 1)
            for n in range(NJ):
                m = P if n % 3 < 2 else NG * D
                pool.wait_ge(s_pm, n + 1)
                pool.tensor_tensor(parts0[n % 3][0:m, 2, :], rest0[n % 3][0:m, :], parts0[n % 3][0:m, 1, :],
                                   ALU.subtract).then_inc(s_pl, 1)
            pool.wait_ge(s_vinit, 2)
            pool.wait_ge(s_vev, NCH)

            def values(u, k):
                pool.tensor_copy(Vs[:, k, :, 0:VW], V_all[:, bass.ds(u, 1), :, :].rearrange("p o n d -> p (o n) d")
                                 ).then_inc(s_vs, 1)

            for u in range(2):
                values(u, u)
            with pool.Fori(0, LOOPS, 1) as it:
                for k in range(STEP):
                    pool.wait_ge(s_pv, it * (STEP * GROUPS) + (k * GROUPS + 3))
                    values(it * STEP + (k + 2), (k + 2) % STEP)

            def inverse_root(c, done, value, out_sem, n_out):
                v = slice(c * TPC, (c + 1) * TPC)
                pool.wait_ge(done, value)
                pool.tensor_scalar(rstd[:, v], mv[:, v, 1], EPS, None, ALU.add).then_inc(s_half, 1)
                pool.wait_ge(s_half, n_out)
                pool.tensor_tensor(rstd[:, v], rstd[:, v], half[:, v], ALU.pow).then_inc(out_sem, 1)

            for c in range(NCH):
                inverse_root(c, s_bn, 2 * TPC * (c + 1), s_rstd, c + 2)

            pool.wait_ge(s_slot, 1)
            pool.wait_ge(s_score, 1)
            pool.wait_ge(s_zf, 32)
            for n in range(NT):
                pool.tensor_scalar(rows[:, n, :], x_all[:, n, :], score[:, n:n + 1], None, ALU.mult).then_inc(s_xsc, 1)
            for n in range(NT):
                pool.wait_ge(s_xsc, n + 1)
                pool.indirect_dma_start(xs_d, bass.IndirectOffsetOnAxis(ap=slot[:, n:n + 1], axis=0), rows[:, n, :],
                                        None).then_inc(s_sc, 16)
            pool.wait_ge(s_sc, 16 * NT)
            for i in range(2):
                pool.wait_ge(s_ys[i], 16 * ((MT + 1 - i) // 2))
            for n in range(NT):
                pool.indirect_dma_start(rows[:, n, :], None, ys_d,
                                        bass.IndirectOffsetOnAxis(ap=slot[:, n:n + 1], axis=0)).then_inc(s_gt[n // TPC], 16)
            for c in range(NCH):
                inverse_root(c, s_bn2, (2 * TPC + 1) * (c + 1), s_rstd2, NCH + c + 2)


def constants():
    bf16 = mybir.dt.np(BF16)
    import numpy as np
    cf = np.zeros((P, CF_N), np.float32)
    cf[:, CF_ID:CF_ID + P] = np.eye(P)
    cf[0:8, CF_SEL:CF_SEL + P] = np.arange(P)[None, :] // D == np.arange(8)[:, None]
    cf[:, CF_IOTA:CF_IOTA + E] = np.arange(E) - E
    cf[:, CF_THR:CF_THR + E * NT] = np.tile(np.arange(NT) * P, E)
    cf[:, CF_LE:CF_LE + E * E] = (np.arange(E)[None, :] <= np.arange(E)[:, None]).ravel()
    cf[:, CF_J:CF_J + MT * E] = np.repeat(np.arange(MT), E)
    big = -3e38
    a = np.arange(P)
    cb = np.zeros((P, CB_N), np.float32)
    cb[:, CB_ID:CB_ID + P] = np.eye(P)
    cb[:, CB_MQK:CB_MQK + P] = np.where(a[None, :] > a[:, None], big, 0)
    cb[:, CB_MKQ:CB_MKQ + HG * P] = np.tile(np.where(a[:, None] > a[None, :], big, 0), (1, HG))
    cb[:, CB_TRI:CB_TRI + P] = a[:, None] < a[None, :]
    cb[:, CB_ONE:CB_ONE + P] = 1
    cb = cb.astype(bf16)
    base = 2.0 ** (-2.0 ** -1)
    slopes = np.array([base * base ** i for i in range(NG)], np.float32).astype(np.float64)
    rest = np.arange(T)[None, :] * slopes[:, None] / SCALE
    al = np.zeros((NG, AL_ROWS, T), bf16)
    for p in range(AL_ROWS):
        al[:, p] = rest.astype(bf16)
        rest = rest - al[:, p].astype(np.float64)
    al = np.concatenate([al.reshape(NG * AL_ROWS, T)] * B)
    one = np.ones((AL_ROWS, HG * T), bf16)
    zero = np.zeros((M_ROWS, HG * T), bf16)
    return {"cf": cf, "cb": cb, "al": al, "one": one, "zero": zero}


def kernel(L0_attn_x, L0_attn_Wq, L0_attn_Wk, L0_attn_Wv, L0_attn_Wo, L0_ffn_router_w, L0_ffn_gate_up_proj,
           L0_ffn_down_proj, L0_ffn_shared_gate_w, L0_ffn_shared_up_w, L0_ffn_shared_down_w):
    import numpy as np
    import concourse.bacc as bacc
    from concourse.bass_utils import run_bass_kernel_spmd
    x = np.ascontiguousarray(L0_attn_x).reshape(NTOK, C)
    arrays = {
        "x": x, "xT": np.ascontiguousarray(x.T), "wq": L0_attn_Wq, "wk": L0_attn_Wk, "wv": L0_attn_Wv,
        "wo": L0_attn_Wo, "rt": np.ascontiguousarray(np.asarray(L0_ffn_router_w).T), "gu": L0_ffn_gate_up_proj,
        "dn": L0_ffn_down_proj, "sg": L0_ffn_shared_gate_w, "su": L0_ffn_shared_up_w, "sd": L0_ffn_shared_down_w,
    }
    arrays = {n: np.ascontiguousarray(a) for n, a in arrays.items()} | constants()
    nc = bacc.Bacc("TRN2", target_bir_lowering=False, num_devices=1)
    aps = [nc.dram_tensor(f"in_{n}", a.shape, mybir.dt.from_np(a.dtype), kind="ExternalInput").ap()
           for n, a in arrays.items()]
    out = nc.dram_tensor("out", (NTOK, C), F32, kind="ExternalOutput").ap()
    layer(nc, *aps, out)
    r = run_bass_kernel_spmd(nc, [{f"in_{n}": a for n, a in arrays.items()}], core_ids=[0])
    return r.results[0]["out"].reshape(B, T, C)
```

```python
import concourse.bass as bass
from concourse import mybir
from contextlib import ExitStack

F32 = mybir.dt.float32
BF16 = mybir.dt.bfloat16
I32 = mybir.dt.int32
ALU = mybir.AluOpType
ACT = mybir.ActivationFunctionType
AX = mybir.AxisListType

P = 128
B, T, C = 2, 1024, 256
NTOK = B * T
NH, NG, D = 16, 4, 16
HG = NH // NG
NU = B * NG
E, H, I = 8, 256, 512
KC = C // P
NT = NTOK // P
CH = 512
NCH = NTOK // CH
TPC = CH // P
FC = I // P
NQ = T // P
M_ROWS, AL_ROWS = 3, 4
ROW0 = M_ROWS + AL_ROWS
Q_PART = (0, 0, 0, 1, 1, 2)
K_PART = (0, 1, 2, 0, 1, 0)
K_RUNS = ((0, 3), (3, 2), (5, 1))
KROWS = ROW0 + D * len(Q_PART)
SCALE = float(D) ** -0.5
EPS = 1e-5
MT = NTOK // P + E - 1
VW = D + 1
VP = 32
STEP = 3
LOOPS = (NU - 2) // STEP
assert LOOPS * STEP == NU - 2

CF_ID, CF_SEL, CF_IOTA, CF_THR, CF_LE, CF_J = 0, 128, 256, 264, 392, 456
CF_TOK = CF_J + MT * E
CF_N = CF_TOK + NT
CB_ID, CB_MQK, CB_MKQ, CB_TRI, CB_ONE = 0, 128, 256, 768, 896
CB_N = 1024


def row_max_tiles():
    tiles = []
    for qi in range(NQ):
        w = min(qi + 1, 4) * P
        heads = [[0, 1, 2, 3]] if qi == 0 else [[0, 1], [2], [3]] if qi == 1 else [[h] for h in range(HG)]
        tiles += [(qi, hs[0], len(hs), 0, w, False) for hs in heads]
        if qi >= 4:
            w = (qi - 3) * P
            per = max(1, 4 * P // w) if w != 3 * P else 1
            tiles += [(qi, h, per, 4 * P, w, True) for h in range(0, HG, per)]
    return tiles


def prob_group(s):
    return [(j, 0, j, s) if s <= j else (j, 1, NQ - 1 - j, s - j - 1) for j in range(4)]


def first_tiles(n):
    lots = 3 * NCH - FIRST_A
    i = n - FIRST_A
    return range(i * (NA - 1) // lots, (i + 1) * (NA - 1) // lots)


FIRST_A = 9
A_TILES = row_max_tiles()
NA = len(A_TILES) + 1
GROUPS = 9
assert NA % 2 == 0 and GROUPS % STEP == 0


def layer(nc, x_d, xT_d, wq_d, wk_d, wv_d, wo_d, rt_d, gu_d, dn_d, sg_d, su_d, sd_d, cf_d, cb_d, al_d, one_d, zero_d,
          out_d):
    with ExitStack() as ctx:
        def sb(name, shape, dt=F32):
            return ctx.enter_context(nc.sbuf_tensor(name, shape, dt))

        def sem(name):
            return ctx.enter_context(nc.semaphore(name))

        qparts_d = nc.dram_tensor("qparts", [3, NU * HG * D, T], BF16, kind="Internal").ap()
        kparts_d = nc.dram_tensor("kparts", [3, NU * D, T], BF16, kind="Internal").ap()
        yT_d = nc.dram_tensor("yT", [NU * HG * D, T], F32, kind="Internal").ap()
        den_d = nc.dram_tensor("den", [NU * HG, T], F32, kind="Internal").ap()
        rden_d = nc.dram_tensor("rden", [NU * HG, T], F32, kind="Internal").ap()
        xs_d = nc.dram_tensor("xs", [MT * P, C + 1], F32, kind="Internal").ap()
        acc_d = nc.dram_tensor("acc", [NTOK + 2, C], F32, kind="Internal").ap()

        ps = ctx.enter_context(nc.psum_tensor("ps", [P, 8, 512], F32))

        wgu = sb("wgu", [P, E * KC * 2 * I])
        qk_or_dn = sb("qk_or_dn", [P, E * FC * H])
        qk16 = qk_or_dn[:, :].bitcast(BF16)
        Q6 = [qk16[:, i * HG * T:(i + 1) * HG * T].rearrange("p (h t) -> p h t", h=HG) for i in range(STEP)]
        k_at = STEP * HG * T
        K6 = [qk16[:, k_at + i * T:k_at + (i + 1) * T] for i in range(STEP)]
        wdn = qk_or_dn
        wsg = sb("wsg", [P, KC, I])
        wsu = sb("wsu", [P, KC, I])
        wsd = sb("wsd", [P, FC, H])
        x_all = sb("x_all", [P, NT, C])
        probs = sb("probs", [P, 3 * 4, 512])
        pr2 = probs[:, :, :].rearrange("p a b -> p (a b)")
        xTc = pr2[:, 0:NCH * KC * CH].rearrange("p (c k t) -> p c k t", c=NCH, k=KC)
        x1T = pr2[:, 0:KC * NTOK].rearrange("p (k t) -> p k t", k=KC)
        rows = sb("rows", [P, NT, C + 1])
        V_all = sb("V_all", [P, NU, NQ, VW])
        Vs = sb("Vs", [P, STEP, NQ, VP])
        yU = sb("yU", [P, 2, 512])
        wq = yU[:, 0, :].rearrange("p (k n) -> p k n", k=KC)
        wkv = yU[:, 1, 0:KC * P].rearrange("p (k n) -> p k n", k=KC)
        wo = sb("wo", [P, KC, C])
        rt = sb("rt", [P, KC, E])
        cf = sb("cf", [P, CF_N])
        cb = sb("cb", [P, CB_N], BF16)
        tmp = sb("tmp", [P, 4096 + 2 * (C + 1)])
        t16 = tmp[:, 0:3 * 3 * CH // 2].bitcast(BF16)
        parts0 = [t16[:, r * 3 * CH:(r + 1) * 3 * CH].rearrange("p (a t) -> p a t", a=3) for r in range(3)]
        vT = tmp[NG * D:P, 3840:3840 + CH]
        rest0 = [tmp[:, 2304 + r * CH:2304 + (r + 1) * CH] for r in range(3)]
        yTc = [tmp[:, i * 1024:(i + 1) * 1024].rearrange("p (k t) -> p k t", k=KC) for i in range(2)]
        rdc = [tmp[0:8, 2048 + i * 1024:2048 + (i + 1) * 1024].rearrange("p (k t) -> p k t", k=KC) for i in range(2)]
        den = tmp[:, 4096:4096 + 256]
        hT = tmp[:, 0:2048].rearrange("p (f t) -> p f t", f=FC)
        sG = [tmp[:, 2048 + i * 512:2048 + (i + 1) * 512] for i in range(2)]
        esG = [tmp[:, i * 512:(i + 1) * 512] for i in range(2)]
        eh = [tmp[:, 1024 + i * 512:1024 + (i + 1) * 512] for i in range(2)]
        ehT = [tmp[:, 2048 + i * 512:2048 + (i + 1) * 512].rearrange("p (f t) -> p f t", f=FC) for i in range(2)]
        xs = [tmp[:, 4096 + i * (C + 1):4096 + (i + 1) * (C + 1)] for i in range(2)]
        xsT = [tmp[:, 3584 + i * 256:3584 + (i + 1) * 256].rearrange("p (k t) -> p k t", k=KC) for i in range(2)]
        z = [rows[:, i, 0:C] for i in range(2)]

        mx0 = sb("mx0", [P, HG, NQ])
        mx1 = sb("mx1", [P, HG, 4])
        mrest = sb("mrest", [P, HG * NQ])
        mparts = sb("mparts", [P, 3, HG * NQ], BF16)
        mrow = sb("mrow", [3 * HG * NQ, P], BF16)
        credit = sb("credit", [1, 8])
        bst = sb("bst", [P, NT, 6])
        mv = sb("mv", [P, NT, 2])
        rstd = sb("rstd", [P, NT])
        half = sb("half", [P, NT])
        lg = sb("lg", [P, NT, E])
        top = sb("top", [P, NT])
        eq = sb("eq", [P, NT, E])
        first = sb("first", [P, NT])
        oh = sb("oh", [P, NT, E])
        oh16 = sb("oh16", [P, NT, E], BF16)
        score = sb("score", [P, NT])
        many = sb("many", [P, E, NT])
        cnt = sb("cnt", [P, E])
        cum = sb("cum", [P, E, E])
        end = sb("end", [P, E])
        start = sb("start", [P, E])
        place = sb("place", [P, NT, E])
        slotf = sb("slotf", [P, NT])
        slot = sb("slot", [P, NT], I32)
        after = sb("after", [P, MT, E])
        etf = sb("etf", [P, MT])
        et = sb("et", [P, MT], I32)
        tok = sb("tok", [P, MT], I32)
        tokj = [sb(f"tokj{i}", [P, 1], I32) for i in range(2)]
        zst = [sb(f"zst{i}", [P, 6]) for i in range(2)]
        zmv = [sb(f"zmv{i}", [P, 2]) for i in range(2)]
        zrs = [sb(f"zrs{i}", [P, 1]) for i in range(2)]

        idf = cf[:, CF_ID:CF_ID + P]
        sel = cf[0:8, CF_SEL:CF_SEL + P]
        id16 = cb[:, CB_ID:CB_ID + P]
        mask_qk = cb[:, CB_MQK:CB_MQK + P]
        mask_kq = cb[:, CB_MKQ:CB_MKQ + HG * P]
        tri = cb[:, CB_TRI:CB_TRI + P]
        ones = cb[:, CB_ONE:CB_ONE + P]

        s_w0, s_x, s_wo, s_wsh, s_wgu, s_wdn = (sem(n) for n in ("s_w0", "s_x", "s_wo", "s_wsh", "s_wgu", "s_wdn"))
        s_xT = [sem(f"s_xT{i}") for i in range(NCH)]
        s_prj, s_ph, s_pr, s_pm, s_pl, s_vT, s_vps, s_vev = (
            sem(n) for n in ("s_prj", "s_ph", "s_pr", "s_pm", "s_pl", "s_vT", "s_vps", "s_vev"))
        s_pw = [sem(f"s_pw{i}") for i in range(3)]
        s_one, s_seen = sem("s_one"), sem("s_seen")
        s_qk = [sem(f"s_qk{i}") for i in range(STEP)]
        s_vinit, s_vs = sem("s_vinit"), sem("s_vs")
        s_aps, s_amax, s_split, s_mparts, s_mrow = (
            sem(n) for n in ("s_aps", "s_amax", "s_split", "s_mparts", "s_mrow"))
        s_st, s_exp, s_pv, s_yev = (sem(n) for n in ("s_st", "s_exp", "s_pv", "s_yev"))
        s_yst = [sem(f"s_yst{i}") for i in range(2)]
        s_den, s_rd, s_rds = sem("s_den"), sem("s_rd"), sem("s_rds")
        s_ch = [sem(f"s_ch{i}") for i in range(2)]
        s_rb, s_yn, s_op, s_res, s_bn, s_rstd, s_x1, s_tp, s_x1T, s_lg = (
            sem(n) for n in ("s_rb", "s_yn", "s_op", "s_res", "s_bn", "s_rstd", "s_x1", "s_tp", "s_x1T", "s_lg"))
        s_half = sem("s_half")
        s_zero, s_zf = sem("s_zero"), sem("s_zf")
        s_rt, s_oh, s_rank, s_ez, s_score, s_slot, s_xsc = (
            sem(n) for n in ("s_rt", "s_oh", "s_rank", "s_ez", "s_score", "s_slot", "s_xsc"))
        s_sc = sem("s_sc")
        s_g, s_u, s_sg, s_h, s_dn, s_acc = (sem(n) for n in ("s_g", "s_u", "s_sg", "s_h", "s_dn", "s_acc"))
        s_xs = [sem(f"s_xs{i}") for i in range(2)]
        s_et, s_ete, s_eg, s_eu, s_es, s_eh, s_eht, s_ehe, s_ed = (
            sem(n) for n in ("s_et", "s_ete", "s_eg", "s_eu", "s_es", "s_eh", "s_eht", "s_ehe", "s_ed"))
        s_accd, s_tok, s_tokj = (sem(n) for n in ("s_accd", "s_tok", "s_tokj"))
        s_zin = [sem(f"s_zin{i}") for i in range(2)]
        s_z, s_zst, s_zmv, s_zrs, s_fin, s_pseen, s_vseen = (
            sem(n) for n in ("s_z", "s_zst", "s_zmv", "s_zrs", "s_fin", "s_pseen", "s_vseen"))
        s_out = [sem(f"s_out{i}") for i in range(2)]

        NJ = 3 * NCH
        S_QK = 16 * (2 + len(Q_PART) + len(K_RUNS))

        block = ctx.enter_context(nc.Block())

        @block.sync
        def _(sp):
            def wait_for(sem, value):
                sp.wait_ge(sem, value)
                sp.sem_inc(s_seen, 1)

            def load_unit(u, i):
                sp.dma_start(Q6[i][0:M_ROWS, :, :].rearrange("p h t -> p (h t)"), zero_d).then_inc(s_qk[i], 16)
                sp.dma_start(K6[i][M_ROWS:ROW0, :], al_d[bass.ds(u * AL_ROWS, AL_ROWS), :]).then_inc(s_qk[i], 16)
                for s, part in enumerate(Q_PART):
                    r = ROW0 + s * D
                    sp.dma_start(Q6[i][r:r + D, :, :], qparts_d[part, bass.ds(u * HG * D, HG * D), :]
                                 .rearrange("(h d) t -> d h t", h=HG)).then_inc(s_qk[i], 16)
                for s, n in K_RUNS:
                    r = ROW0 + s * D
                    sp.dma_start(K6[i][r:r + n * D, :], kparts_d[0:n, bass.ds(u * D, D), :]).then_inc(s_qk[i], 16)

            def store_y(u, bank):
                wait_for(s_yev, u * 2 + (bank + 1 + 2))
                for j in range(4):
                    qi = j if bank == 0 else NQ - 1 - j
                    src = yU[32 * j:32 * j + VW, bank, :].rearrange("p (h t) -> p h t", h=HG)
                    sp.dma_start(yT_d[bass.ds(u * HG * D, HG * D), qi * P:(qi + 1) * P]
                                 .rearrange("(h d) t -> d h t", h=HG), src[0:D]).then_inc(s_yst[bank], 16)
                    sp.dma_start(den_d[bass.ds(u * HG, HG), qi * P:(qi + 1) * P]
                                 .rearrange("(o h) t -> o h t", o=1), src[D:VW]).then_inc(s_yst[bank], 16)

            def max_rows(u, i):
                sp.wait_ge(s_amax, u * NA + NA)
                n = HG * NQ
                for p in range(3):
                    sp.dma_start(Q6[i][p:p + 1, :, :].rearrange("o h t -> o (h t)")
                                 .rearrange("o (a b) -> o a b", a=n),
                                 mrow[p * n:(p + 1) * n, :]).then_inc(s_mrow, 16)

            def load_den(b):
                sp.dma_start(den[:, b * P:(b + 1) * P], den_d[b * NH:(b + 1) * NH, :]
                             .rearrange("a (b t) -> (a b) t", t=P)).then_inc(s_den, 16)

            def store_rden(b):
                sp.wait_ge(s_rd, b + 1)
                sp.dma_start(rden_d[b * NH:(b + 1) * NH, :].rearrange("a (b t) -> (a b) t", t=P),
                             den[:, b * P:(b + 1) * P]).then_inc(s_rds, 16)
                sp.wait_ge(s_rds, 16 * (b + 1))

            def load_yT(c):
                b, col = c // 2, (c % 2) * CH
                sp.dma_start(yTc[c % 2], yT_d[b * C:(b + 1) * C, col:col + CH]
                             .rearrange("(k p) t -> p k t", p=P)).then_inc(s_ch[c % 2], 16)

            def load_rden(c):
                b, col = c // 2, (c % 2) * CH
                sp.dma_start(rdc[c % 2], rden_d[b * NH:(b + 1) * NH, col:col + CH]
                             .rearrange("(k p) t -> p k t", p=8)).then_inc(s_ch[c % 2], 16)

            def step(u, k, last=False, more=True):
                if more:
                    sp.wait_ge(s_pv, u * GROUPS + 3)
                    load_unit(u + 2, (k + 2) % STEP)
                store_y(u, 0)
                if not last:
                    max_rows(u + 1, (k + 1) % STEP)
                store_y(u, 1)

            def load_x(c):
                sp.dma_start(xTc[:, c], xT_d[:, c * CH:(c + 1) * CH].rearrange("(k p) t -> p k t", p=P)
                             ).then_inc(s_xT[c], 16)

            load_x(0)
            sp.dma_start(wq, wq_d.rearrange("(k p) n -> p k n", p=P)).then_inc(s_w0, 16)
            sp.dma_start(wkv[:, :, 0:NG * D], wk_d.rearrange("(k p) n -> p k n", p=P)).then_inc(s_w0, 16)
            sp.dma_start(wkv[:, :, NG * D:P], wv_d.rearrange("(k p) n -> p k n", p=P)).then_inc(s_w0, 16)
            load_x(1)
            sp.dma_start(cf[:], cf_d).then_inc(s_w0, 16)
            sp.dma_start(cb[:], cb_d).then_inc(s_w0, 16)
            load_x(2)
            load_x(3)
            for i in range(STEP):
                sp.dma_start(Q6[i][M_ROWS:ROW0, :, :].rearrange("p h t -> p (h t)"), one_d).then_inc(s_one, 16)
                sp.dma_start(K6[i][0:M_ROWS, :], one_d[0:M_ROWS, 0:T]).then_inc(s_one, 16)
            for n in range(NJ):
                sp.wait_ge(s_pl, n + 1)
                c, k = n // 3, n % 3
                b, col = c // 2, (c % 2) * CH
                if k < 2:
                    r, m, dst = b * NH * D + k * P, P, qparts_d
                else:
                    r, m, dst = b * NG * D, NG * D, kparts_d
                sp.dma_start(dst[:, r:r + m, col:col + CH].rearrange("a r t -> r a t"),
                             parts0[n % 3][0:m, :, :]).then_inc(s_pw[n % 3], 16)
                if n == NJ // 2:
                    for i in range(3):
                        sp.wait_ge(s_pw[i], 16 * NJ // 6)
                    load_unit(0, 0)
                if n == NJ - 3:
                    load_unit(1, 1)
            for i in range(3):
                sp.wait_ge(s_pw[i], 16 * NJ // 3)
            max_rows(0, 0)
            with sp.Fori(0, LOOPS, 1) as it:
                for k in range(STEP):
                    step(it * STEP + k, k)
            for u in range(LOOPS * STEP, NU):
                step(u, u % STEP, last=(u == NU - 1), more=False)
                if u == NU - 2:
                    load_den(0)
                    store_rden(0)
                    for c in range(2):
                        load_yT(c)
                        load_rden(c)

            for i in range(2):
                sp.wait_ge(s_yst[i], 128 * (NU + 1))
            load_den(1)
            for e in range(E):
                sp.dma_start(wdn[:, e * FC * H:(e + 1) * FC * H].rearrange("p (f n) -> p f n", f=FC),
                             dn_d[e].rearrange("(f p) n -> p f n", p=P)).then_inc(s_wdn, 16)
            for c in range(2, NCH):
                sp.wait_ge(s_op, TPC * (c - 1))
                load_yT(c)
                if c == 2:
                    store_rden(1)
                load_rden(c)

            acc_t = acc_d[0:NTOK, :].rearrange("(n p) c -> p n c", p=P)
            for c in range(NCH):
                v = slice(c * TPC, (c + 1) * TPC)
                sp.wait_ge(s_acc, TPC * (c + 1))
                sp.dma_start(acc_t[:, v, :], x_all[:, v, :]).then_inc(s_accd, 16)

            def load_tile(j, k):
                sp.dma_start(xs[k], xs_d[bass.ds(j * P, P), :]).then_inc(s_xs[k], 16)

            sp.wait_ge(s_sc, 16 * NT)
            load_tile(0, 0)
            load_tile(1, 1)

            def next_tile(j, k):
                wait_for(s_tok, j + 1)
                load_tile(j + 2, k)

            with sp.Fori(0, (MT - 3) // 2, 1) as it:
                for k in range(2):
                    next_tile(it * 2 + k, k)
            next_tile(MT - 3, (MT - 3) % 2)
            sp.wait_ge(s_zf, 48)
            sp.wait_ge(s_accd, 16 * NCH)
            for i in range(2):
                sp.wait_ge(s_out[i], 16 * ((MT + 1 - i) // 2))

        @block.tensor
        def _(pe):
            pe.wait_ge(s_w0, 16 * 5)
            def job(n):
                c, k = n // 3, n % 3
                pe.wait_ge(s_xT[c], 16)
                if n >= 4:
                    pe.wait_ge(s_pr, n - 3)
                if n >= 6 and (n - 4) % 3 == 2:
                    pe.wait_ge(s_vT, (n - 4) // 3 + 1)
                for kc in range(KC):
                    w = wq[:, kc, k * P:(k + 1) * P] if k < 2 else wkv[:, kc, :]
                    mm = pe.matmul(ps[:, 4 + n % 4, :], w, xTc[:, c, kc, :], start=kc == 0, stop=kc == KC - 1)
                mm.then_inc(s_prj, 1)

            def values(c):
                pe.wait_ge(s_vT, c + 1)
                if c >= 2:
                    pe.wait_ge(s_vev, c - 1)
                for t in range(TPC):
                    mm = pe.transpose(ps[:, 2 + c % 2, t * NG * D:(t + 1) * NG * D], vT[:, t * P:(t + 1) * P],
                                      cf[NG * D:P, CF_ID + NG * D:CF_ID + P])
                mm.then_inc(s_vps, 1)

            def max_tile(u, k, t):
                bank = t % 2
                if isinstance(u, int) and u == 0:
                    if t >= 2:
                        pe.wait_ge(s_amax, t - 1)
                else:
                    pe.wait_ge(s_amax, u * NA + t - 1)
                if t == NA - 1:
                    pe.wait_ge(s_mparts, u + 1)
                    pe.transpose(ps[0:3 * HG * NQ, bank, 0:P // 2].bitcast(BF16),
                                 mparts[:, :, :].rearrange("p a b -> p (a b)"), id16).then_inc(s_aps, 1)
                    return
                qi, h0, nh, k0, w, _ = A_TILES[t]
                diag = qi * P - k0
                for i in range(nh):
                    q = Q6[k][0:KROWS, h0 + i, qi * P:(qi + 1) * P]
                    o = ps[:, bank, i * w:(i + 1) * w]
                    masked = diag < w
                    mm = pe.matmul(o, q, K6[k][0:KROWS, k0:k0 + w], start=True, stop=not masked)
                    if masked:
                        mm = pe.matmul(o[:, diag:diag + P], id16, mask_qk, start=False, stop=True)
                mm.then_inc(s_aps, 1)

            def scores(u, k, s):
                for j, bank, qi, kb in prob_group(s):
                    if j % 2 == 0:
                        pe.wait_ge(s_exp, u * (2 * GROUPS) + 2 * s + j // 2 + 1)
                    o = ps[:, 4 + j, :]
                    if kb == qi:
                        pe.matmul(o, id16, mask_kq, start=True, stop=False)
                    mm = pe.matmul(o, K6[k][0:KROWS, kb * P:(kb + 1) * P],
                                   Q6[k][0:KROWS, :, qi * P:(qi + 1) * P], start=kb != qi, stop=True)
                    if j % 2 == 1:
                        mm.then_inc(s_st, 1)

            def weigh(u, k, s):
                pe.wait_ge(s_exp, u * (2 * GROUPS) + 2 * s + 4)
                if s <= 1:
                    pe.wait_ge(s_yev, u * 2 + s + 1)
                for j, bank, qi, kb in prob_group(s):
                    mm = pe.matmul(ps[32 * j:32 * j + VP, 2 + bank, :], Vs[:, k, kb, :], probs[:, 4 * (s % 3) + j, :],
                                   start=kb == 0, stop=kb == qi, skip_group_check=True)
                mm.then_inc(s_pv, 1)

            def step(u, k, last=False):
                todo = [] if last else list(range(NA))
                if not last:
                    pe.wait_ge(s_qk[(k + 1) % STEP], S_QK * NEXT(u, k))

                def some(n):
                    n = max(n, 0)
                    for t in todo[:n]:
                        max_tile(u + 1, (k + 1) % STEP, t)
                    del todo[:n]

                some(4)
                pe.wait_ge(s_mrow, u * 48 + 48)
                pe.wait_ge(s_vs, u + 1)
                for s in range(GROUPS):
                    scores(u, k, s)
                    some(min(3, len(todo) - 1) if s < GROUPS - 1 else 1)
                    if s:
                        weigh(u, k, s - 1)
                    if s < GROUPS - 1:
                        some(min(2, len(todo) - 1))
                weigh(u, k, GROUPS - 1)

            def NEXT(u, k):
                if isinstance(u, int):
                    return (u + 1) // STEP + 1
                return IT[0] + (2 if k == STEP - 1 else 1)

            IT = [None]
            for n in range(NJ):
                job(n)
                if n % 3 == 0 and n:
                    values(n // 3 - 1)
                if n == FIRST_A:
                    pe.wait_ge(s_one, 32 * STEP)
                    pe.wait_ge(s_qk[0], S_QK)
                if n >= FIRST_A:
                    for t in first_tiles(n):
                        max_tile(0, 0, t)
            values(NCH - 1)
            max_tile(0, 0, NA - 1)
            with pe.Fori(0, LOOPS, 1) as it:
                IT[0] = it
                for k in range(STEP):
                    step(it * STEP + k, k)
            for u in range(LOOPS * STEP, NU):
                step(u, u % STEP, last=u == NU - 1)

            def project(c):
                pe.wait_ge(s_ch[c % 2], 32 * (c // 2 + 1))
                if c >= 1:
                    pe.wait_ge(s_yn, c)
                for kc in range(KC):
                    mm = pe.matmul(ps[:, kc, :], sel, rdc[c % 2][:, kc, :], start=True, stop=True)
                mm.then_inc(s_rb, 1)
                pe.wait_ge(s_yn, c + 1)
                for t in range(TPC):
                    n = c * TPC + t
                    if n >= 2:
                        pe.wait_ge(s_res, n - 1)
                    for kc in range(KC):
                        mm = pe.matmul(ps[:, 2 + n % 2, 0:C], yTc[c % 2][:, kc, t * P:(t + 1) * P], wo[:, kc, :],
                                       start=kc == 0, stop=kc == KC - 1)
                    mm.then_inc(s_op, 1)

            def route(c):
                pe.wait_ge(s_x1, c + 1)
                if c >= 1:
                    pe.wait_ge(s_x1T, KC * c)
                for kc in range(KC):
                    for t in range(TPC):
                        mm = pe.transpose(ps[:, 4 + kc, t * P:(t + 1) * P],
                                          x_all[:, c * TPC + t, kc * P:(kc + 1) * P], idf)
                    mm.then_inc(s_tp, 1)
                pe.wait_ge(s_x1T, KC * (c + 1))
                for t in range(TPC):
                    n = c * TPC + t
                    for kc in range(KC):
                        mm = pe.matmul(ps[:, 6, n * E:(n + 1) * E], x1T[:, kc, n * P:(n + 1) * P], rt[:, kc, :],
                                       start=kc == 0, stop=kc == KC - 1)
                mm.then_inc(s_lg, 1)

            pe.wait_ge(s_wo, 32)
            pe.wait_ge(s_yev, 2 * NU + 2)
            project(0)
            for c in range(NCH):
                if c + 1 < NCH:
                    project(c + 1)
                route(c)

            def gate_up(n):
                c, f = n // FC, n % FC
                if n >= 2:
                    pe.wait_ge(s_h, n - 1)
                for w, bank, done in ((wsg, 0, s_g), (wsu, 1, s_u)):
                    for kc in range(KC):
                        mm = pe.matmul(ps[:, bank + 2 * (n % 2), :], w[:, kc, f * P:(f + 1) * P],
                                       x1T[:, kc, c * CH:(c + 1) * CH], start=kc == 0, stop=kc == KC - 1)
                    mm.then_inc(done, 1)

            def down(c):
                pe.wait_ge(s_h, FC * (c + 1))
                for t in range(TPC):
                    n = c * TPC + t
                    if n >= 2:
                        pe.wait_ge(s_acc, n - 1)
                    for f in range(FC):
                        mm = pe.matmul(ps[:, 4 + n % 2, 0:H], hT[:, f, t * P:(t + 1) * P], wsd[:, f, :],
                                       start=f == 0, stop=f == FC - 1)
                    mm.then_inc(s_dn, 1)

            pe.wait_ge(s_wsh, 48)
            pe.wait_ge(s_res, NT)
            gate_up(0)
            gate_up(1)
            pe.wait_ge(s_oh, 1)
            flat = oh16[:, :, :].rearrange("p n e -> p (n e)")
            pe.matmul(ps[:, 7, 0:NT * E], tri, flat, start=True, stop=False, skip_group_check=True)
            for n in range(NT - 1):
                later = ps[:, 7, (n + 1) * E:NT * E].rearrange("p (n e) -> p n e", e=E)
                pe.matmul(later, ones, oh16[:, n:n + 1, :].broadcast_to([P, NT - 1 - n, E]), start=False,
                          stop=n == NT - 2, skip_group_check=True)
            for n in range(NT):
                mm = pe.matmul(ps[:, 6, 256:256 + E], ones, oh16[:, n, :], start=n == 0, stop=n == NT - 1)
            mm.then_inc(s_rank, 1)
            gate_up(2)
            gate_up(3)
            for c in range(NCH):
                if c + 1 < NCH:
                    gate_up(FC * (c + 1))
                    gate_up(FC * (c + 1) + 1)
                down(c)
                if c + 1 < NCH:
                    gate_up(FC * (c + 1) + 2)
                    gate_up(FC * (c + 1) + 3)

            def rows_T(j, k):
                pe.wait_ge(s_xs[k], (j // 2 + 1) * 16 if isinstance(j, int) else IT[0] * 16 + 32)
                if not isinstance(j, int) or j >= 1:
                    pe.wait_ge(s_ete, j)
                for kc in range(KC):
                    mm = pe.transpose(ps[:, 6, kc * P:(kc + 1) * P], xs[k][:, kc * P:(kc + 1) * P], idf)
                mm.then_inc(s_et, 1)

            def expert_up(j, k):
                e = pe.value_load(et[0:1, bass.ds(j, 1)], min_val=0, max_val=E - 1)
                pe.wait_ge(s_ete, j + 1)
                if not isinstance(j, int) or j >= 2:
                    pe.wait_ge(s_eh, j - 1)
                for half_i, done in ((0, s_eg), (1, s_eu)):
                    for kc in range(KC):
                        mm = pe.matmul(ps[:, 2 * k + half_i, :], xsT[k][:, kc, :],
                                       wgu[:, bass.ds(e * (KC * 2 * I) + (kc * 2 * I + half_i * I), I)],
                                       start=kc == 0, stop=kc == KC - 1)
                    mm.then_inc(done, 1)

            def hidden_T(j, k):
                pe.wait_ge(s_eh, j + 1)
                if not isinstance(j, int) or j >= 2:
                    pe.wait_ge(s_ehe, j - 1)
                for f in range(FC):
                    mm = pe.transpose(ps[:, 4 + k, f * P:(f + 1) * P], eh[k][:, f * P:(f + 1) * P], idf)
                mm.then_inc(s_eht, 1)

            def expert_down(j, k):
                e = pe.value_load(et[0:1, bass.ds(j, 1)], min_val=0, max_val=E - 1)
                pe.wait_ge(s_ehe, j + 1)
                if not isinstance(j, int) or j >= 1:
                    pe.wait_ge(s_z, j)
                for f in range(FC):
                    mm = pe.matmul(ps[:, 7, 0:H], ehT[k][:, f, :], wdn[:, bass.ds(e * (FC * H) + f * H, H)],
                                   start=f == 0, stop=f == FC - 1)
                mm.then_inc(s_ed, 1)

            def expert_step(j, k):
                hidden_T(j, k)
                if not isinstance(j, int) or j + 2 < MT:
                    rows_T(j + 2, k)
                if not isinstance(j, int) or j + 1 < MT:
                    expert_up(j + 1, 1 - k)
                expert_down(j, k)

            pe.wait_ge(s_wgu, 16 * E)
            pe.wait_ge(s_wdn, 16 * E)
            pe.wait_ge(s_slot, 1)
            pe.wait_ge(s_acc, NT)
            rows_T(0, 0)
            rows_T(1, 1)
            expert_up(0, 0)
            for j in range(2):
                expert_step(j, j)
            with pe.Fori(1, (MT - 3) // 2, 1) as it:
                IT[0] = it
                for k in range(2):
                    expert_step(it * 2 + k, k)
            for j in range(MT - 3, MT):
                expert_step(j, j % 2)

        @block.scalar
        def _(act):
            def put_values(c):
                act.wait_ge(s_vps, c + 1)
                b = c // 2
                for t in range(TPC):
                    kb = (c % 2) * TPC + t
                    ins = act.activation(V_all[:, b * NG:(b + 1) * NG, kb, 0:D],
                                         ps[:, 2 + c % 2, t * NG * D:(t + 1) * NG * D].rearrange("p (g d) -> p g d", g=NG),
                                         ACT.Copy)
                ins.then_inc(s_vev, 1)

            later_loads = [(x_all[:], x_d, s_x), (wo[:], wo_d, s_wo), (rt[:], rt_d, s_wo), (wsg[:], sg_d, s_wsh),
                           (wsu[:], su_d, s_wsh), (wsd[:], sd_d, s_wsh)]
            for n in range(NJ):
                c, k = n // 3, n % 3
                m = P if k < 2 else NG * D
                act.wait_ge(s_prj, n + 1)
                if n >= 3:
                    act.wait_ge(s_pw[n % 3], 16 * (n // 3))
                act.activation(parts0[n % 3][0:m, 0, :], ps[0:m, 4 + n % 4, :], ACT.Copy).then_inc(s_ph, 1)
                if n < len(later_loads):
                    dst, src, done = later_loads[n]
                    act.dma_start(dst, src.rearrange("(k p) n -> p k n", p=P)).then_inc(done, 16)
                if k == 2:
                    if c >= 1:
                        act.wait_ge(s_vps, c)
                    act.activation(vT, ps[NG * D:P, 4 + n % 4, :], ACT.Copy).then_inc(s_vT, 1)
                if k == 0 and c:
                    put_values(c - 1)
            put_values(NCH - 1)
            def load_gate_up(e):
                act.dma_start(wgu[:, e * KC * 2 * I:(e + 1) * KC * 2 * I].rearrange("p (k n) -> p k n", k=KC),
                              gu_d[e].rearrange("(k p) n -> p k n", p=P)).then_inc(s_wgu, 16)

            def zero_slots():
                act.wait_ge(s_zero, 3)
                xs_t = xs_d.rearrange("(n p) c -> p n c", p=P)
                act.dma_start(xs_t[:, 0:NT, :], rows[:]).then_inc(s_zf, 16)
                act.dma_start(xs_t[:, NT:MT, :], rows[:, 0:MT - NT, :]).then_inc(s_zf, 16)
                act.dma_start(acc_d[NTOK:NTOK + 2, :], rows[0:2, 0, 0:C]).then_inc(s_zf, 16)

            def step(u, k):
                for s in range(GROUPS):
                    if isinstance(u, int) and u == NU - 2 and s < 5:
                        load_gate_up(s)
                    if isinstance(u, int) and u == NU - 1 and s < E - 5:
                        load_gate_up(5 + s)
                    if isinstance(u, int) and u == NU - 1 and s == E - 5:
                        zero_slots()
                    for hb in range(2):
                        act.wait_ge(s_st, u * (2 * GROUPS) + 2 * s + hb + 1)
                        if hb == 0:
                            act.wait_ge(s_pv, u * GROUPS + s + 1)
                        act.activation(probs[:, 4 * (s % 3) + 2 * hb:4 * (s % 3) + 2 * hb + 2, :],
                                       ps[:, 4 + 2 * hb:6 + 2 * hb, :], ACT.Exp, scale=SCALE).then_inc(s_exp, 1)
                    if s == 4:
                        act.wait_ge(s_pv, u * GROUPS + 4 + 3)
                        act.wait_ge(s_yst[0], u * 128 + 128)
                        act.activation(yU[:, 0, :], ps[:, 2, :], ACT.Copy).then_inc(s_yev, 1)
                act.wait_ge(s_pv, u * GROUPS + GROUPS + 3)
                act.wait_ge(s_yst[1], u * 128 + 128)
                act.activation(yU[:, 1, :], ps[:, 3, :], ACT.Copy).then_inc(s_yev, 1)

            with act.Fori(0, LOOPS, 1) as it:
                for k in range(STEP):
                    step(it * STEP + k, k)
            for u in range(LOOPS * STEP, NU):
                step(u, u % STEP)

            for c in range(NCH):
                for kc in range(KC):
                    act.wait_ge(s_tp, KC * c + kc + 1)
                    act.activation(x1T[:, kc, c * CH:(c + 1) * CH], ps[:, 4 + kc, :], ACT.Copy).then_inc(s_x1T, 1)
            act.wait_ge(s_rt, 2)
            act.activation(score[:], top[:], ACT.Exp, scale=-1.0).then_inc(s_ez, 1)
            for n in range(NCH * FC):
                act.wait_ge(s_g, n + 1)
                if n >= 2:
                    act.wait_ge(s_h, n - 1)
                act.activation(sG[n % 2], ps[:, 2 * (n % 2), :], ACT.Silu).then_inc(s_sg, 1)

            def rows_T(j, k):
                act.wait_ge(s_et, j + 1)
                if not isinstance(j, int) or j >= 2:
                    act.wait_ge(s_eu, j - 1)
                act.activation(xsT[k].rearrange("p k t -> p (k t)"), ps[:, 6, 0:C], ACT.Copy).then_inc(s_ete, 1)
                act.activation(tok[:, bass.ds(j, 1)], xs[k][:, C:C + 1], ACT.Copy).then_inc(s_tok, 1)

            def silu(j, k):
                act.wait_ge(s_eg, j + 1)
                if not isinstance(j, int) or j >= 2:
                    act.wait_ge(s_eh, j - 1)
                act.activation(esG[k], ps[:, 2 * k, :], ACT.Silu).then_inc(s_es, 1)

            def hidden_T(j, k):
                act.wait_ge(s_eht, j + 1)
                if not isinstance(j, int) or j >= 2:
                    act.wait_ge(s_ed, j - 1)
                act.activation(ehT[k].rearrange("p f t -> p (f t)"), ps[:, 4 + k, :], ACT.Copy).then_inc(s_ehe, 1)

            def expert_step(j, k):
                hidden_T(j, k)
                if not isinstance(j, int) or j + 2 < MT:
                    rows_T(j + 2, k)
                if not isinstance(j, int) or j + 1 < MT:
                    silu(j + 1, 1 - k)

            rows_T(0, 0)
            rows_T(1, 1)
            silu(0, 0)
            for j in range(2):
                expert_step(j, j)
            with act.Fori(1, (MT - 3) // 2, 1) as it:
                for k in range(2):
                    expert_step(it * 2 + k, k)
            for j in range(MT - 3, MT):
                expert_step(j, j % 2)

        @block.vector
        def _(dve):
            def reduce_tile(u, t):
                qi, h0, nh, k0, w, second = A_TILES[t]
                dve.wait_ge(s_aps, u * NA + t + 1)
                o = mx1[:, h0:h0 + nh, qi - 4] if second else mx0[:, h0:h0 + nh, qi]
                dve.tensor_reduce(o, ps[:, t % 2, 0:nh * w].rearrange("p (h w) -> p h w", h=nh), AX.X,
                                  ALU.max).then_inc(s_amax, 1)

            for n in range(NJ):
                m = P if n % 3 < 2 else NG * D
                h, md, rest = parts0[n % 3][0:m, 0, :], parts0[n % 3][0:m, 1, :], rest0[n % 3][0:m, :]
                dve.wait_ge(s_ph, n + 1)
                if n >= 3:
                    dve.wait_ge(s_pl, n - 2)
                dve.tensor_tensor(rest, ps[0:m, 4 + n % 4, :], h, ALU.subtract).then_inc(s_pr, 1)
                dve.wait_ge(s_pr, n + 1)
                dve.tensor_copy(md, rest).then_inc(s_pm, 1)
                if n >= FIRST_A:
                    for t in first_tiles(n):
                        reduce_tile(0, t)
            dve.wait_ge(s_vev, NCH)
            dve.memset(credit[:, 0:1], 0.0).then_inc(s_exp, 2)
            dve.memset(credit[:, 1:2], 0.0).then_inc(s_pv, 3)
            dve.memset(credit[:, 2:3], 0.0).then_inc(s_yev, 2)
            dve.memset(credit[:, 3:4], 0.0).then_inc(s_yst[0], 128)
            dve.memset(credit[:, 4:5], 0.0).then_inc(s_yst[1], 128)

            def row_max(u):
                first_unit = isinstance(u, int) and u == 0
                if not first_unit:
                    dve.wait_ge(s_mparts, u)
                    for t in range(NA - 1):
                        reduce_tile(u, t)
                dve.wait_ge(s_amax, u * NA + NA - 1)
                dve.tensor_tensor(mx0[:, :, 4:NQ], mx0[:, :, 4:NQ], mx1[:], ALU.max).then_inc(s_split, 1)
                dve.wait_ge(s_split, u * 4 + 1)
                m = mx0[:, :, :].rearrange("p h q -> p (h q)")
                dve.tensor_scalar(mparts[:, 0, :], m, -1.0, None, ALU.mult).then_inc(s_split, 1)
                dve.wait_ge(s_split, u * 4 + 2)
                dve.scalar_tensor_tensor(mrest[:], m, -1.0, mparts[:, 0, :], ALU.mult, ALU.subtract).then_inc(s_split, 1)
                dve.wait_ge(s_split, u * 4 + 3)
                dve.tensor_copy(mparts[:, 1, :], mrest[:]).then_inc(s_split, 1)
                dve.wait_ge(s_split, u * 4 + 4)
                dve.tensor_tensor(mparts[:, 2, :], mrest[:], mparts[:, 1, :], ALU.subtract).then_inc(s_mparts, 1)
                dve.wait_ge(s_aps, u * NA + NA)
                if not first_unit:
                    dve.wait_ge(s_mrow, u * 48)
                dve.tensor_copy(mrow[:], ps[0:3 * HG * NQ, (NA - 1) % 2, 0:P // 2].bitcast(BF16)).then_inc(s_amax, 1)

            row_max(0)
            with dve.Fori(0, LOOPS, 1) as it:
                for k in range(STEP):
                    row_max(it * STEP + (k + 1))
            for u in range(LOOPS * STEP, NU - 1):
                row_max(u + 1)

            def invert(b):
                dve.wait_ge(s_den, 16 * (b + 1))
                dve.reciprocal(den[:, b * P:(b + 1) * P], den[:, b * P:(b + 1) * P]).then_inc(s_rd, 1)

            invert(0)

            def normalise(c):
                dve.wait_ge(s_rb, c + 1)
                y = yTc[c % 2].rearrange("p k t -> p (k t)")
                dve.tensor_tensor(y, y, ps[:, 0:KC, :].rearrange("p k t -> p (k t)"), ALU.mult).then_inc(s_yn, 1)

            def residual(c):
                for n in range(c * TPC, (c + 1) * TPC):
                    dve.wait_ge(s_op, n + 1)
                    dve.tensor_tensor(x_all[:, n, :], ps[:, 2 + n % 2, 0:C], x_all[:, n, :], ALU.add).then_inc(s_res, 1)

            def stats(c, done, base):
                for n in range(c * TPC, (c + 1) * TPC):
                    dve.bn_stats(bst[:, n, :], x_all[:, n, :]).then_inc(done, 1)
                for i, n in enumerate(range(c * TPC, (c + 1) * TPC)):
                    dve.wait_ge(done, base + i + 1)
                    ins = dve.bn_aggr(mv[:, n, :], bst[:, n, :]).then_inc(done, 1)

            def scale_rows(c):
                for n in range(c * TPC, (c + 1) * TPC):
                    ins = dve.tensor_scalar(x_all[:, n, :], x_all[:, n, :], mv[:, n, 0:1], rstd[:, n:n + 1],
                                            ALU.subtract, ALU.mult)
                return ins

            dve.wait_ge(s_x, 16)
            normalise(0)
            invert(1)
            for c in range(NCH):
                residual(c)
                dve.wait_ge(s_res, TPC * (c + 1))
                stats(c, s_bn, 2 * TPC * c)
                if c + 1 < NCH:
                    normalise(c + 1)
                dve.wait_ge(s_rstd, c + 1)
                scale_rows(c).then_inc(s_x1, 1)

            count = [0]

            def chain(ins):
                count[0] += 1
                ins.then_inc(s_rt, 1)
                dve.wait_ge(s_rt, count[0])

            def over_e(ap):
                return ap.rearrange("p (n o) -> p n o", o=1).broadcast_to([P, NT, E])

            iota = cf[:, CF_IOTA:CF_IOTA + E].rearrange("p (o e) -> p o e", o=1).broadcast_to([P, NT, E])
            dve.wait_ge(s_lg, NCH)
            chain(dve.tensor_copy(lg[:, :, :].rearrange("p n e -> p (n e)"), ps[:, 6, 0:NT * E]))
            chain(dve.tensor_reduce(top[:], lg[:], AX.X, ALU.max))
            chain(dve.tensor_tensor(eq[:], lg[:], over_e(top[:]), ALU.is_equal))
            chain(dve.tensor_tensor(eq[:], eq[:], iota, ALU.mult))
            chain(dve.tensor_reduce(first[:], eq[:], AX.X, ALU.min))
            chain(dve.tensor_tensor(oh[:], iota, over_e(first[:]), ALU.is_equal))
            dve.tensor_copy(oh16[:], oh[:]).then_inc(s_oh, 1)
            dve.wait_ge(s_ez, 1)
            chain(dve.tensor_scalar(score[:], score[:], 1.0, None, ALU.add))
            dve.reciprocal(score[:], score[:]).then_inc(s_score, 1)
            dve.wait_ge(s_rank, 1)
            chain(dve.tensor_copy(cnt[:], ps[:, 6, 256:256 + E]))
            chain(dve.tensor_tensor(many[:], cnt[:, :].rearrange("p (e o) -> p e o", o=1).broadcast_to([P, E, NT]),
                                    cf[:, CF_THR:CF_THR + E * NT].rearrange("p (e n) -> p e n", e=E), ALU.is_gt))
            chain(dve.tensor_reduce(cnt[:], many[:], AX.X, ALU.add))
            chain(dve.tensor_tensor(cum[:], cnt[:, :].rearrange("p (o e) -> p o e", o=1).broadcast_to([P, E, E]),
                                    cf[:, CF_LE:CF_LE + E * E].rearrange("p (a b) -> p a b", a=E), ALU.mult))
            chain(dve.tensor_reduce(end[:], cum[:], AX.X, ALU.add))
            chain(dve.tensor_tensor(start[:], end[:], cnt[:], ALU.subtract))
            chain(dve.tensor_scalar(start[:], start[:], float(P), None, ALU.mult))
            chain(dve.tensor_tensor(place[:], ps[:, 7, 0:NT * E].rearrange("p (n e) -> p n e", e=E),
                                    start[:, :].rearrange("p (o e) -> p o e", o=1).broadcast_to([P, NT, E]), ALU.add))
            chain(dve.tensor_tensor(place[:], place[:], oh[:], ALU.mult))
            chain(dve.tensor_reduce(slotf[:], place[:], AX.X, ALU.add))
            chain(dve.tensor_copy(slot[:], slotf[:]))
            chain(dve.tensor_tensor(after[:], cf[:, CF_J:CF_J + MT * E].rearrange("p (j e) -> p j e", e=E),
                                    end[:, :].rearrange("p (o e) -> p o e", o=1).broadcast_to([P, MT, E]), ALU.is_ge))
            chain(dve.tensor_reduce(etf[:], after[:], AX.X, ALU.add))
            chain(dve.tensor_scalar(etf[:], etf[:], float(E - 1), None, ALU.min))
            dve.tensor_copy(et[:], etf[:]).then_inc(s_slot, 1)

            def hidden(n):
                c, f = n // FC, n % FC
                dve.wait_ge(s_sg, n + 1)
                dve.wait_ge(s_u, n + 1)
                if f == 0 and c >= 1:
                    dve.wait_ge(s_dn, TPC * c)
                dve.tensor_tensor(hT[:, f, :], sG[n % 2], ps[:, 2 * (n % 2) + 1, :], ALU.mult).then_inc(s_h, 1)

            for n in range(FC):
                hidden(n)
            for c in range(NCH):
                for n in range(c * TPC, (c + 1) * TPC):
                    dve.wait_ge(s_dn, n + 1)
                    dve.wait_ge(s_xsc, n + 2)
                    dve.tensor_tensor(x_all[:, n, :], ps[:, 4 + n % 2, 0:H], x_all[:, n, :], ALU.add).then_inc(s_acc, 1)
                if c + 1 < NCH:
                    for n in range(FC):
                        hidden(FC * (c + 1) + n)

            def hidden_rows(j, k):
                dve.wait_ge(s_es, j + 1)
                dve.wait_ge(s_eu, j + 1)
                if not isinstance(j, int) or j >= 2:
                    dve.wait_ge(s_eht, j - 1)
                dve.tensor_tensor(eh[k], esG[k], ps[:, 2 * k + 1, :], ALU.mult).then_inc(s_eh, 1)

            def finish(j, k):
                dve.wait_ge(s_ed, j + 1)
                dve.wait_ge(s_zin[k], (j // 2 + 1) * 16 if isinstance(j, int) else IT[0] * 16 + 16)
                dve.tensor_tensor(z[k], ps[:, 7, 0:H], z[k], ALU.add).then_inc(s_z, 1)
                dve.wait_ge(s_z, j + 1)
                dve.bn_stats(zst[k][:], z[k]).then_inc(s_zst, 1)
                dve.wait_ge(s_zst, j + 1)
                dve.sem_inc(s_vseen, 1)
                dve.bn_aggr(zmv[k][:], zst[k][:]).then_inc(s_zmv, 1)
                dve.wait_ge(s_zmv, j + 1)
                dve.wait_ge(s_zrs, 2 * j + 2)
                dve.tensor_scalar(z[k], z[k], zmv[k][:, 0:1], zrs[k][:], ALU.subtract, ALU.mult).then_inc(s_fin, 1)

            def expert_step(j, k):
                if not isinstance(j, int) or j + 1 < MT:
                    hidden_rows(j + 1, 1 - k)
                finish(j, k)

            IT = [None]
            hidden_rows(0, 0)
            for j in range(2):
                expert_step(j, j)
            with dve.Fori(1, (MT - 3) // 2, 1) as it:
                IT[0] = it
                for k in range(2):
                    expert_step(it * 2 + k, k)
            for j in range(MT - 3, MT):
                expert_step(j, j % 2)

        @block.gpsimd
        def _(pool):
            pool.memset(V_all[:, :, :, D:VW], 1.0).then_inc(s_vinit, 1)
            pool.memset(Vs[:], 0.0).then_inc(s_vinit, 1)
            pool.memset(rows[:, :, 0:C], 0.0).then_inc(s_zero, 1)
            for i in range(2):
                pool.memset(rows[:, i::2, C:C + 1], float(NTOK + i)).then_inc(s_zero, 1)
            pool.memset(half[:], -0.5).then_inc(s_half, 1)
            for n in range(NJ):
                m = P if n % 3 < 2 else NG * D
                pool.wait_ge(s_pm, n + 1)
                pool.tensor_tensor(parts0[n % 3][0:m, 2, :], rest0[n % 3][0:m, :], parts0[n % 3][0:m, 1, :],
                                   ALU.subtract).then_inc(s_pl, 1)
            pool.wait_ge(s_vinit, 2)
            pool.wait_ge(s_vev, NCH)

            def values(u, k):
                pool.tensor_copy(Vs[:, k, :, 0:VW], V_all[:, bass.ds(u, 1), :, :].rearrange("p o n d -> p (o n) d")
                                 ).then_inc(s_vs, 1)

            for u in range(2):
                values(u, u)
            with pool.Fori(0, LOOPS, 1) as it:
                for k in range(STEP):
                    pool.wait_ge(s_pv, it * (STEP * GROUPS) + (k * GROUPS + 3))
                    values(it * STEP + (k + 2), (k + 2) % STEP)

            def inverse_root(c, done, value, out_sem, n_out):
                v = slice(c * TPC, (c + 1) * TPC)
                pool.wait_ge(done, value)
                pool.tensor_scalar(rstd[:, v], mv[:, v, 1], EPS, None, ALU.add).then_inc(s_half, 1)
                pool.wait_ge(s_half, n_out)
                pool.tensor_tensor(rstd[:, v], rstd[:, v], half[:, v], ALU.pow).then_inc(out_sem, 1)

            for c in range(NCH):
                inverse_root(c, s_bn, 2 * TPC * (c + 1), s_rstd, c + 2)

            pool.wait_ge(s_slot, 1)
            pool.wait_ge(s_score, 1)
            pool.wait_ge(s_zf, 48)
            pool.tensor_copy(rows[:, :, C], cf[:, CF_TOK:CF_TOK + NT]).then_inc(s_xsc, 1)
            for n in range(NT):
                pool.tensor_scalar(rows[:, n, 0:C], x_all[:, n, :], score[:, n:n + 1], None, ALU.mult).then_inc(s_xsc, 1)
            for n in range(NT):
                pool.wait_ge(s_xsc, n + 2)
                pool.indirect_dma_start(xs_d, bass.IndirectOffsetOnAxis(ap=slot[:, n:n + 1], axis=0), rows[:, n, :],
                                        None).then_inc(s_sc, 16)
            pool.wait_ge(s_sc, 16 * NT)
            pool.wait_ge(s_accd, 16 * NCH)

            def wait_for(sem, value):
                pool.wait_ge(sem, value)
                pool.sem_inc(s_pseen, 1)

            def fetch(j, k):
                wait_for(s_tok, j + 1)
                pool.tensor_copy(tokj[k][:], tok[:, bass.ds(j, 1)]).then_inc(s_tokj, 1)
                wait_for(s_tokj, j + 1)
                pool.indirect_dma_start(z[k], None, acc_d, bass.IndirectOffsetOnAxis(ap=tokj[k][:], axis=0)
                                        ).then_inc(s_zin[k], 16)

            def finish(j, k):
                wait_for(s_zmv, j + 1)
                pool.tensor_scalar(zrs[k][:], zmv[k][:, 1:2], EPS, None, ALU.add).then_inc(s_zrs, 1)
                pool.wait_ge(s_zrs, 2 * j + 1)
                pool.tensor_tensor(zrs[k][:], zrs[k][:], half[:, 0:1], ALU.pow).then_inc(s_zrs, 1)
                wait_for(s_fin, j + 1)
                pool.indirect_dma_start(out_d, bass.IndirectOffsetOnAxis(ap=tokj[k][:], axis=0), z[k], None
                                        ).then_inc(s_out[k], 16)

            def expert_step(j, k):
                finish(j, k)
                if not isinstance(j, int) or j + 2 < MT:
                    wait_for(s_out[k], (j // 2 + 1) * 16 if isinstance(j, int) else IT[0] * 16 + 16)
                    fetch(j + 2, k)

            IT = [None]
            for j in range(2):
                fetch(j, j)
            for j in range(2):
                expert_step(j, j)
            with pool.Fori(1, (MT - 3) // 2, 1) as it:
                IT[0] = it
                for k in range(2):
                    expert_step(it * 2 + k, k)
            for j in range(MT - 3, MT):
                expert_step(j, j % 2)


def constants():
    bf16 = mybir.dt.np(BF16)
    import numpy as np
    cf = np.zeros((P, CF_N), np.float32)
    cf[:, CF_ID:CF_ID + P] = np.eye(P)
    cf[0:8, CF_SEL:CF_SEL + P] = np.arange(P)[None, :] // D == np.arange(8)[:, None]
    cf[:, CF_IOTA:CF_IOTA + E] = np.arange(E) - E
    cf[:, CF_THR:CF_THR + E * NT] = np.tile(np.arange(NT) * P, E)
    cf[:, CF_LE:CF_LE + E * E] = (np.arange(E)[None, :] <= np.arange(E)[:, None]).ravel()
    cf[:, CF_J:CF_J + MT * E] = np.repeat(np.arange(MT), E)
    cf[:, CF_TOK:CF_TOK + NT] = np.arange(NT)[None, :] * P + np.arange(P)[:, None]
    big = -3e38
    a = np.arange(P)
    cb = np.zeros((P, CB_N), np.float32)
    cb[:, CB_ID:CB_ID + P] = np.eye(P)
    cb[:, CB_MQK:CB_MQK + P] = np.where(a[None, :] > a[:, None], big, 0)
    cb[:, CB_MKQ:CB_MKQ + HG * P] = np.tile(np.where(a[:, None] > a[None, :], big, 0), (1, HG))
    cb[:, CB_TRI:CB_TRI + P] = a[:, None] < a[None, :]
    cb[:, CB_ONE:CB_ONE + P] = 1
    cb = cb.astype(bf16)
    base = 2.0 ** (-2.0 ** -1)
    slopes = np.array([base * base ** i for i in range(NG)], np.float32).astype(np.float64)
    rest = np.arange(T)[None, :] * slopes[:, None] / SCALE
    al = np.zeros((NG, AL_ROWS, T), bf16)
    for p in range(AL_ROWS):
        al[:, p] = rest.astype(bf16)
        rest = rest - al[:, p].astype(np.float64)
    al = np.concatenate([al.reshape(NG * AL_ROWS, T)] * B)
    one = np.ones((AL_ROWS, HG * T), bf16)
    zero = np.zeros((M_ROWS, HG * T), bf16)
    return {"cf": cf, "cb": cb, "al": al, "one": one, "zero": zero}


def kernel(L0_attn_x, L0_attn_Wq, L0_attn_Wk, L0_attn_Wv, L0_attn_Wo, L0_ffn_router_w, L0_ffn_gate_up_proj,
           L0_ffn_down_proj, L0_ffn_shared_gate_w, L0_ffn_shared_up_w, L0_ffn_shared_down_w):
    import numpy as np
    import concourse.bacc as bacc
    from concourse.bass_utils import run_bass_kernel_spmd
    x = np.ascontiguousarray(L0_attn_x).reshape(NTOK, C)
    arrays = {
        "x": x, "xT": np.ascontiguousarray(x.T), "wq": L0_attn_Wq, "wk": L0_attn_Wk, "wv": L0_attn_Wv,
        "wo": L0_attn_Wo, "rt": np.ascontiguousarray(np.asarray(L0_ffn_router_w).T), "gu": L0_ffn_gate_up_proj,
        "dn": L0_ffn_down_proj, "sg": L0_ffn_shared_gate_w, "su": L0_ffn_shared_up_w, "sd": L0_ffn_shared_down_w,
    }
    arrays = {n: np.ascontiguousarray(a) for n, a in arrays.items()} | constants()
    nc = bacc.Bacc("TRN2", target_bir_lowering=False, num_devices=1)
    aps = [nc.dram_tensor(f"in_{n}", a.shape, mybir.dt.from_np(a.dtype), kind="ExternalInput").ap()
           for n, a in arrays.items()]
    out = nc.dram_tensor("out", (NTOK + 2, C), F32, kind="ExternalOutput").ap()
    layer(nc, *aps, out)
    r = run_bass_kernel_spmd(nc, [{f"in_{n}": a for n, a in arrays.items()}], core_ids=[0])
    return r.results[0]["out"][:NTOK].reshape(B, T, C)
```

```python
import concourse.bass as bass
from concourse import mybir
from contextlib import ExitStack

F32 = mybir.dt.float32
BF16 = mybir.dt.bfloat16
I32 = mybir.dt.int32
ALU = mybir.AluOpType
ACT = mybir.ActivationFunctionType
AX = mybir.AxisListType

P = 128
B, T, C = 2, 1024, 256
NTOK = B * T
NH, NG, D = 16, 4, 16
HG = NH // NG
NU = B * NG
E, H, I = 8, 256, 512
KC = C // P
NT = NTOK // P
CH = 512
NCH = NTOK // CH
TPC = CH // P
FC = I // P
NQ = T // P
M_ROWS, AL_ROWS = 3, 4
ROW0 = M_ROWS + AL_ROWS
Q_PART = (0, 0, 0, 1, 1, 2)
K_PART = (0, 1, 2, 0, 1, 0)
K_RUNS = ((0, 3), (3, 2), (5, 1))
KROWS = ROW0 + D * len(Q_PART)
SCALE = float(D) ** -0.5
EPS = 1e-5
MT = NTOK // P + E - 1
VW = D + 1
VP = 32
STEP = 3
LOOPS = (NU - 2) // STEP
assert LOOPS * STEP == NU - 2

CF_ID, CF_SEL, CF_IOTA, CF_THR, CF_LE, CF_J = 0, 128, 256, 264, 392, 456
CF_TOK = CF_J + MT * E
CF_N = CF_TOK + NT
CB_ID, CB_MQK, CB_MKQ, CB_TRI, CB_ONE = 0, 128, 256, 768, 896
CB_N = 1024


def row_max_tiles():
    tiles = []
    for qi in range(NQ):
        w = min(qi + 1, 4) * P
        heads = [[0, 1, 2, 3]] if qi == 0 else [[0, 1], [2], [3]] if qi == 1 else [[h] for h in range(HG)]
        tiles += [(qi, hs[0], len(hs), 0, w, False) for hs in heads]
        if qi >= 4:
            w = (qi - 3) * P
            per = max(1, 4 * P // w) if w != 3 * P else 1
            tiles += [(qi, h, per, 4 * P, w, True) for h in range(0, HG, per)]
    return tiles


def prob_group(s):
    return [(j, 0, j, s) if s <= j else (j, 1, NQ - 1 - j, s - j - 1) for j in range(4)]


def first_tiles(n):
    lots, i = len(JOBS) - FIRST_A, n - FIRST_A
    return range(i * (NA - 1) // lots, (i + 1) * (NA - 1) // lots)


JOBS = [(c, k) for c in (0, 1) for k in (0, 2)] + [(0, 1), (1, 1)] + [(c, k) for c in (2, 3) for k in (0, 2)] + [
    (2, 1), (3, 1)]
NJ = len(JOBS)
UNIT0_JOBS = 4
FIRST_A = 8
A_TILES = row_max_tiles()
NA = len(A_TILES) + 1
GROUPS = 9
LOT = (1, 2, 2)
assert NA % 2 == 0 and GROUPS % STEP == 0


def layer(nc, x_d, xT_d, wq_d, wk_d, wv_d, wo_d, rt_d, gu_d, dn_d, sg_d, su_d, sd_d, cf_d, cb_d, al_d, one_d, zero_d,
          out_d):
    with ExitStack() as ctx:
        def sb(name, shape, dt=F32):
            return ctx.enter_context(nc.sbuf_tensor(name, shape, dt))

        def sem(name):
            return ctx.enter_context(nc.semaphore(name))

        qparts_d = nc.dram_tensor("qparts", [3, NU * HG * D, T], BF16, kind="Internal").ap()
        kparts_d = nc.dram_tensor("kparts", [3, NU * D, T], BF16, kind="Internal").ap()
        yT_d = nc.dram_tensor("yT", [2, 4, VP, B * NH, P], F32, kind="Internal").ap()
        rden_d = nc.dram_tensor("rden", [B, 2, 4, NH, P], F32, kind="Internal").ap()
        xs_d = nc.dram_tensor("xs", [MT * P, C + 1], F32, kind="Internal").ap()
        acc_d = nc.dram_tensor("acc", [NTOK + 2, C], F32, kind="Internal").ap()

        ps = ctx.enter_context(nc.psum_tensor("ps", [P, 8, 512], F32))

        wgu = sb("wgu", [P, E * KC * 2 * I])
        qk_or_dn = sb("qk_or_dn", [P, E * FC * H])
        qk16 = qk_or_dn[:, :].bitcast(BF16)
        Q6 = [qk16[:, i * HG * T:(i + 1) * HG * T].rearrange("p (h t) -> p h t", h=HG) for i in range(STEP)]
        k_at = STEP * HG * T
        K6 = [qk16[:, k_at + i * T:k_at + (i + 1) * T] for i in range(STEP)]
        wdn = qk_or_dn
        wsg = sb("wsg", [P, KC, I])
        wsu = sb("wsu", [P, KC, I])
        wsd = sb("wsd", [P, FC, H])
        x_all = sb("x_all", [P, NT, C])
        probs = sb("probs", [P, 3 * 4, 512])
        pr2 = probs[:, :, :].rearrange("p a b -> p (a b)")
        xTc = pr2[:, 0:NCH * KC * CH].rearrange("p (c k t) -> p c k t", c=NCH, k=KC)
        x1T = pr2[:, 0:KC * NTOK].rearrange("p (k t) -> p k t", k=KC)
        rows = sb("rows", [P, NT, C + 1])
        V_all = sb("V_all", [P, NU, NQ, VW])
        Vs = sb("Vs", [P, STEP, NQ, VP])
        yU = sb("yU", [P, 2, 512])
        wq = yU[:, 0, :].rearrange("p (k n) -> p k n", k=KC)
        wkv = yU[:, 1, 0:KC * P].rearrange("p (k n) -> p k n", k=KC)
        wo = sb("wo", [P, KC, C])
        rt = sb("rt", [P, KC, E])
        cf = sb("cf", [P, CF_N])
        cb = sb("cb", [P, CB_N], BF16)
        tmp = sb("tmp", [P, 4096 + 2 * (C + 1)])
        t16 = tmp[:, 0:3 * 3 * CH // 2].bitcast(BF16)
        parts0 = [t16[:, r * 3 * CH:(r + 1) * 3 * CH].rearrange("p (a t) -> p a t", a=3) for r in range(3)]
        vT = tmp[NG * D:P, 3840:3840 + CH]
        rest0 = [tmp[:, 2304 + r * CH:2304 + (r + 1) * CH] for r in range(3)]
        yTc = [tmp[:, i * 1024:(i + 1) * 1024].rearrange("p (k t) -> p k t", k=KC) for i in range(3)]
        rdc = [tmp[0:NH, 3072 + i * CH:3072 + (i + 1) * CH] for i in range(2)]
        den = tmp[:, 4096:4096 + 256]
        hT = tmp[:, 0:2048].rearrange("p (f t) -> p f t", f=FC)
        hT0 = tmp[:, 3072:3584]
        sG = [tmp[:, 2048 + i * 512:2048 + (i + 1) * 512] for i in range(2)]
        esG = [tmp[:, i * 512:(i + 1) * 512] for i in range(2)]
        eh = [tmp[:, 1024 + i * 512:1024 + (i + 1) * 512] for i in range(2)]
        ehT = [tmp[:, 2048 + i * 512:2048 + (i + 1) * 512].rearrange("p (f t) -> p f t", f=FC) for i in range(2)]
        xs = [tmp[:, 4096 + i * (C + 1):4096 + (i + 1) * (C + 1)] for i in range(2)]
        xsT = [tmp[:, 3584 + i * 256:3584 + (i + 1) * 256].rearrange("p (k t) -> p k t", k=KC) for i in range(2)]
        z = [rows[:, i, 0:C] for i in range(2)]

        mx0 = sb("mx0", [P, HG, NQ])
        mx1 = sb("mx1", [P, HG, 4])
        mrest = sb("mrest", [P, HG * NQ])
        mparts = sb("mparts", [P, 3, HG * NQ], BF16)
        mrow = sb("mrow", [3 * HG * NQ, P], BF16)
        credit = sb("credit", [1, 8])
        bst = sb("bst", [P, NT, 6])
        mv = sb("mv", [P, NT, 2])
        rstd = sb("rstd", [P, NT])
        half = sb("half", [P, NT])
        lg = sb("lg", [P, NT, E])
        top = sb("top", [P, NT])
        eq = sb("eq", [P, NT, E])
        first = sb("first", [P, NT])
        oh = sb("oh", [P, NT, E])
        oh16 = sb("oh16", [P, NT, E], BF16)
        score = sb("score", [P, NT])
        many = sb("many", [P, E, NT])
        cnt = sb("cnt", [P, E])
        cum = sb("cum", [P, E, E])
        end = sb("end", [P, E])
        start = sb("start", [P, E])
        place = sb("place", [P, NT, E])
        slotf = sb("slotf", [P, NT])
        slot = sb("slot", [P, NT], I32)
        after = sb("after", [P, MT, E])
        etf = sb("etf", [P, MT])
        et = sb("et", [P, MT], I32)
        tok = sb("tok", [P, MT], I32)
        tokj = [sb(f"tokj{i}", [P, 1], I32) for i in range(2)]
        zst = [sb(f"zst{i}", [P, 6]) for i in range(2)]
        zmv = [sb(f"zmv{i}", [P, 2]) for i in range(2)]
        zrs = [sb(f"zrs{i}", [P, 1]) for i in range(2)]

        idf = cf[:, CF_ID:CF_ID + P]
        sel = cf[0:NH, CF_SEL:CF_SEL + P]
        def hidden_part(c, f):
            return hT0 if f == 0 and c % 2 else hT[:, f, :]

        id16 = cb[:, CB_ID:CB_ID + P]
        mask_qk = cb[:, CB_MQK:CB_MQK + P]
        mask_kq = cb[:, CB_MKQ:CB_MKQ + HG * P]
        tri = cb[:, CB_TRI:CB_TRI + P]
        ones = cb[:, CB_ONE:CB_ONE + P]

        s_wq, s_w0, s_x, s_wo, s_wsh, s_wgu, s_wdn = (
            sem(n) for n in ("s_wq", "s_w0", "s_x", "s_wo", "s_wsh", "s_wgu", "s_wdn"))
        s_xT = [sem(f"s_xT{i}") for i in range(NCH)]
        s_prj, s_ph, s_pr, s_pm, s_pl, s_vT, s_vps, s_vev = (
            sem(n) for n in ("s_prj", "s_ph", "s_pr", "s_pm", "s_pl", "s_vT", "s_vps", "s_vev"))
        s_pw = [sem(f"s_pw{i}") for i in range(3)]
        s_one, s_seen = sem("s_one"), sem("s_seen")
        s_qk = [sem(f"s_qk{i}") for i in range(STEP)]
        s_vinit, s_vs = sem("s_vinit"), sem("s_vs")
        s_aps, s_amax, s_split, s_mparts, s_mrow = (
            sem(n) for n in ("s_aps", "s_amax", "s_split", "s_mparts", "s_mrow"))
        s_st, s_exp, s_pv, s_yev = (sem(n) for n in ("s_st", "s_exp", "s_pv", "s_yev"))
        s_yst = [sem(f"s_yst{i}") for i in range(2)]
        s_den, s_rd, s_rds = sem("s_den"), sem("s_rd"), sem("s_rds")
        s_ch = [sem(f"s_ch{i}") for i in range(NCH)]
        s_rb, s_yn, s_op, s_res, s_bn, s_rstd, s_x1, s_tp, s_x1T, s_lg = (
            sem(n) for n in ("s_rb", "s_yn", "s_op", "s_res", "s_bn", "s_rstd", "s_x1", "s_tp", "s_x1T", "s_lg"))
        s_half = sem("s_half")
        s_zero, s_zf = sem("s_zero"), sem("s_zf")
        s_rt, s_oh, s_rank, s_ez, s_score, s_slot, s_xsc = (
            sem(n) for n in ("s_rt", "s_oh", "s_rank", "s_ez", "s_score", "s_slot", "s_xsc"))
        s_sc = sem("s_sc")
        s_g, s_u, s_sg, s_h, s_dn, s_acc = (sem(n) for n in ("s_g", "s_u", "s_sg", "s_h", "s_dn", "s_acc"))
        s_xs = [sem(f"s_xs{i}") for i in range(2)]
        s_et, s_ete, s_eg, s_eu, s_es, s_eh, s_eht, s_ehe, s_ed = (
            sem(n) for n in ("s_et", "s_ete", "s_eg", "s_eu", "s_es", "s_eh", "s_eht", "s_ehe", "s_ed"))
        s_accd, s_tok, s_tokj = (sem(n) for n in ("s_accd", "s_tok", "s_tokj"))
        s_zin = [sem(f"s_zin{i}") for i in range(2)]
        s_z, s_zst, s_zmv, s_zrs, s_fin, s_pseen, s_vseen = (
            sem(n) for n in ("s_z", "s_zst", "s_zmv", "s_zrs", "s_fin", "s_pseen", "s_vseen"))
        s_out = [sem(f"s_out{i}") for i in range(2)]

        S_QK = 16 * (2 + len(Q_PART) + len(K_RUNS))

        def a_bank(u, t):
            return t % 3 if isinstance(u, int) and u == 0 and t < NA - 1 else t % 2

        block = ctx.enter_context(nc.Block())

        @block.sync
        def _(sp):
            def wait_for(sem, value):
                sp.wait_ge(sem, value)
                sp.sem_inc(s_seen, 1)

            def load_unit(u, i):
                load_unit_head(u, i)
                load_unit_q(u, i)
                load_unit_k(u, i)

            def load_unit_head(u, i):
                sp.dma_start(Q6[i][0:M_ROWS, :, :].rearrange("p h t -> p (h t)"), zero_d).then_inc(s_qk[i], 16)
                sp.dma_start(K6[i][M_ROWS:ROW0, :], al_d[bass.ds(u * AL_ROWS, AL_ROWS), :]).then_inc(s_qk[i], 16)

            def load_unit_q(u, i):
                for s, part in enumerate(Q_PART):
                    r = ROW0 + s * D
                    sp.dma_start(Q6[i][r:r + D, :, :], qparts_d[part, bass.ds(u * HG * D, HG * D), :]
                                 .rearrange("(h d) t -> d h t", h=HG)).then_inc(s_qk[i], 16)

            def load_unit_k(u, i):
                for s, n in K_RUNS:
                    r = ROW0 + s * D
                    sp.dma_start(K6[i][r:r + n * D, :], kparts_d[0:n, bass.ds(u * D, D), :]).then_inc(s_qk[i], 16)

            def store_y(u, bank):
                wait_for(s_yev, u * 2 + (bank + 1 + 2))
                sp.dma_start(yT_d[bank].rearrange("j d h t -> (j d) h t")[:, bass.ds(u * HG, HG), :],
                             yU[:, bank, :].rearrange("p (h t) -> p h t", h=HG)).then_inc(s_yst[bank], 16)

            def max_rows(u, i):
                sp.wait_ge(s_amax, u * NA + NA)
                n = HG * NQ
                for p in range(3):
                    sp.dma_start(Q6[i][p:p + 1, :, :].rearrange("o h t -> o (h t)")
                                 .rearrange("o (a b) -> o a b", a=n),
                                 mrow[p * n:(p + 1) * n, :]).then_inc(s_mrow, 16)

            def load_den(b):
                sp.dma_start(den[:, b * P:(b + 1) * P],
                             yT_d[:, :, D, b * NH:(b + 1) * NH, :].rearrange("a j h t -> (a j) h t")
                             ).then_inc(s_den, 16)

            def store_rden(b):
                sp.wait_ge(s_rd, b + 1)
                sp.dma_start(rden_d[b].rearrange("a j h t -> (a j h) t"),
                             den[:, b * P:(b + 1) * P]).then_inc(s_rds, 16)
                sp.wait_ge(s_rds, 16 * (b + 1))

            def load_yT(c):
                b, n = c // 2, D // KC
                for kc in range(KC):
                    for j in range(TPC):
                        sp.dma_start(yTc[c % 3][:, kc, j * P:(j + 1) * P],
                                     yT_d[c % 2, j, kc * n:(kc + 1) * n, b * NH:(b + 1) * NH, :]
                                     ).then_inc(s_ch[c], 16)

            def load_rden(c):
                sp.dma_start(rdc[c % 2].rearrange("h (j t) -> h j t", j=TPC),
                             rden_d[c // 2, c % 2].rearrange("j h t -> h j t")).then_inc(s_ch[c], 16)

            def step(u, k, last=False, more=True):
                if more:
                    sp.wait_ge(s_pv, u * GROUPS + 3)
                    load_unit(u + 2, (k + 2) % STEP)
                store_y(u, 0)
                if not last:
                    max_rows(u + 1, (k + 1) % STEP)
                store_y(u, 1)

            def load_x(c):
                sp.dma_start(xTc[:, c], xT_d[:, c * CH:(c + 1) * CH].rearrange("(k p) t -> p k t", p=P)
                             ).then_inc(s_xT[c], 16)

            load_x(0)
            sp.dma_start(wq, wq_d.rearrange("(k p) n -> p k n", p=P)).then_inc(s_wq, 16)
            sp.dma_start(wkv[:, :, 0:NG * D], wk_d.rearrange("(k p) n -> p k n", p=P)).then_inc(s_w0, 16)
            sp.dma_start(wkv[:, :, NG * D:P], wv_d.rearrange("(k p) n -> p k n", p=P)).then_inc(s_w0, 16)
            load_x(1)
            sp.dma_start(cf[:], cf_d).then_inc(s_w0, 16)
            sp.dma_start(cb[:], cb_d).then_inc(s_w0, 16)
            load_x(2)
            load_x(3)
            for i in range(STEP):
                sp.dma_start(Q6[i][M_ROWS:ROW0, :, :].rearrange("p h t -> p (h t)"), one_d).then_inc(s_one, 16)
                sp.dma_start(K6[i][0:M_ROWS, :], one_d[0:M_ROWS, 0:T]).then_inc(s_one, 16)
            for n in range(NJ):
                sp.wait_ge(s_pl, n + 1)
                c, k = JOBS[n]
                b, col = c // 2, (c % 2) * CH
                if k < 2:
                    r, m, dst = b * NH * D + k * P, P, qparts_d
                else:
                    r, m, dst = b * NG * D, NG * D, kparts_d
                sp.dma_start(dst[:, r:r + m, col:col + CH].rearrange("a r t -> r a t"),
                             parts0[n % 3][0:m, :, :]).then_inc(s_pw[n % 3], 16)
                if n == UNIT0_JOBS:
                    for i in range(3):
                        sp.wait_ge(s_pw[i], 16 * ((UNIT0_JOBS + 2 - i) // 3))
                    load_unit_head(0, 0)
                    load_unit_k(0, 0)
                if n == UNIT0_JOBS + 1:
                    load_unit_q(0, 0)
                if n == FIRST_A:
                    load_unit_head(1, 1)
                    load_unit_k(1, 1)
                if n == FIRST_A + 1:
                    load_unit_q(1, 1)
            for i in range(3):
                sp.wait_ge(s_pw[i], 16 * NJ // 3)
            max_rows(0, 0)
            with sp.Fori(0, LOOPS, 1) as it:
                for k in range(STEP):
                    step(it * STEP + k, k)
            for u in range(LOOPS * STEP, NU):
                step(u, u % STEP, last=(u == NU - 1), more=False)
                if u == NU - 2:
                    load_den(0)
                    store_rden(0)
                    for c in range(2):
                        load_yT(c)
                        load_rden(c)

            for i in range(2):
                sp.wait_ge(s_yst[i], 16 * (NU + 1))
            load_den(1)
            load_yT(2)
            store_rden(1)
            for c in range(2, NCH):
                if c == 3:
                    sp.wait_ge(s_op, TPC)
                    load_yT(c)
                sp.wait_ge(s_rb, c - 1)
                load_rden(c)
            for e in range(E):
                sp.dma_start(wdn[:, e * FC * H:(e + 1) * FC * H].rearrange("p (f n) -> p f n", f=FC),
                             dn_d[e].rearrange("(f p) n -> p f n", p=P)).then_inc(s_wdn, 16)

            def load_tile(j, k):
                sp.dma_start(xs[k], xs_d[bass.ds(j * P, P), :]).then_inc(s_xs[k], 16)

            acc_t = acc_d[0:NTOK, :].rearrange("(n p) c -> p n c", p=P)
            for c in range(NCH):
                v = slice(c * TPC, (c + 1) * TPC)
                if c == NCH - 1:
                    sp.wait_ge(s_sc, 16 * NT)
                    load_tile(0, 0)
                    load_tile(1, 1)
                sp.wait_ge(s_acc, TPC * (c + 1))
                sp.dma_start(acc_t[:, v, :], x_all[:, v, :]).then_inc(s_accd, 16)

            def next_tile(j, k):
                wait_for(s_tok, j + 1)
                load_tile(j + 2, k)

            with sp.Fori(0, (MT - 3) // 2, 1) as it:
                for k in range(2):
                    next_tile(it * 2 + k, k)
            next_tile(MT - 3, (MT - 3) % 2)
            sp.wait_ge(s_zf, 48)
            sp.wait_ge(s_accd, 16 * NCH)
            for i in range(2):
                sp.wait_ge(s_out[i], 16 * ((MT + 1 - i) // 2))

        @block.tensor
        def _(pe):
            pe.wait_ge(s_wq, 16)

            def job(n):
                c, k = JOBS[n]
                pe.wait_ge(s_xT[c], 16)
                if n >= 4:
                    pe.wait_ge(s_pr, n - 3)
                    if JOBS[n - 4][1] == 2:
                        pe.wait_ge(s_vT, JOBS[n - 4][0] + 1)
                for kc in range(KC):
                    w = wq[:, kc, k * P:(k + 1) * P] if k < 2 else wkv[:, kc, :]
                    mm = pe.matmul(ps[:, 4 + n % 4, :], w, xTc[:, c, kc, :], start=kc == 0, stop=kc == KC - 1)
                mm.then_inc(s_prj, 1)

            def values(c):
                pe.wait_ge(s_vT, c + 1)
                if c >= 1:
                    pe.wait_ge(s_vev, c)
                for t in range(TPC):
                    mm = pe.transpose(ps[:, 3, t * NG * D:(t + 1) * NG * D], vT[:, t * P:(t + 1) * P],
                                      cf[NG * D:P, CF_ID + NG * D:CF_ID + P])
                mm.then_inc(s_vps, 1)

            def max_tile(u, k, t):
                bank = a_bank(u, t)
                if isinstance(u, int) and u == 0:
                    if t >= 3:
                        pe.wait_ge(s_amax, t - 2)
                else:
                    pe.wait_ge(s_amax, u * NA + t - 1)
                if t == NA - 1:
                    pe.wait_ge(s_mparts, u + 1)
                    pe.transpose(ps[0:3 * HG * NQ, bank, 0:P // 2].bitcast(BF16),
                                 mparts[:, :, :].rearrange("p a b -> p (a b)"), id16).then_inc(s_aps, 1)
                    return
                qi, h0, nh, k0, w, _ = A_TILES[t]
                diag = qi * P - k0
                for i in range(nh):
                    q = Q6[k][0:KROWS, h0 + i, qi * P:(qi + 1) * P]
                    o = ps[:, bank, i * w:(i + 1) * w]
                    masked = diag < w
                    mm = pe.matmul(o, q, K6[k][0:KROWS, k0:k0 + w], start=True, stop=not masked)
                    if masked:
                        mm = pe.matmul(o[:, diag:diag + P], id16, mask_qk, start=False, stop=True)
                mm.then_inc(s_aps, 1)

            def scores(u, k, s, hb):
                for j, bank, qi, kb in prob_group(s)[2 * hb:2 * hb + 2]:
                    if j % 2 == 0:
                        pe.wait_ge(s_exp, u * (2 * GROUPS) + 2 * s + j // 2 + 1)
                    o = ps[:, 4 + j, :]
                    if kb == qi:
                        pe.matmul(o, id16, mask_kq, start=True, stop=False)
                    mm = pe.matmul(o, K6[k][0:KROWS, kb * P:(kb + 1) * P],
                                   Q6[k][0:KROWS, :, qi * P:(qi + 1) * P], start=kb != qi, stop=True)
                    if j % 2 == 1:
                        mm.then_inc(s_st, 1)

            def weigh(u, k, s):
                pe.wait_ge(s_exp, u * (2 * GROUPS) + 2 * s + 4)
                if s <= 1:
                    pe.wait_ge(s_yev, u * 2 + s + 1)
                for j, bank, qi, kb in prob_group(s):
                    mm = pe.matmul(ps[32 * j:32 * j + VP, 2 + bank, :], Vs[:, k, kb, :], probs[:, 4 * (s % 3) + j, :],
                                   start=kb == 0, stop=kb == qi, skip_group_check=True)
                mm.then_inc(s_pv, 1)

            def step(u, k, last=False):
                todo = [] if last else list(range(NA))
                if not last:
                    pe.wait_ge(s_qk[(k + 1) % STEP], S_QK * NEXT(u, k))

                def some(n):
                    n = max(n, 0)
                    for t in todo[:n]:
                        max_tile(u + 1, (k + 1) % STEP, t)
                    del todo[:n]

                some(2)
                pe.wait_ge(s_mrow, u * 48 + 48)
                pe.wait_ge(s_vs, u + 1)
                for s in range(GROUPS):
                    for hb in range(2):
                        scores(u, k, s, hb)
                        some(min(LOT[hb], len(todo) - 1) if s < GROUPS - 1 else hb)
                    if s:
                        weigh(u, k, s - 1)
                    if s < GROUPS - 1:
                        some(min(LOT[2], len(todo) - 1))
                weigh(u, k, GROUPS - 1)

            def NEXT(u, k):
                if isinstance(u, int):
                    return (u + 1) // STEP + 1
                return IT[0] + (2 if k == STEP - 1 else 1)

            IT = [None]
            for n in range(NJ):
                if n == 1:
                    pe.wait_ge(s_w0, 16 * 4)
                job(n)
                if n and JOBS[n - 1][1] == 2:
                    values(JOBS[n - 1][0])
                if n == FIRST_A + 1:
                    pe.wait_ge(s_one, 32 * STEP)
                    pe.wait_ge(s_qk[0], S_QK)
                if n > FIRST_A:
                    for t in first_tiles(n - 1):
                        max_tile(0, 0, t)
            for t in first_tiles(NJ - 1):
                max_tile(0, 0, t)
            max_tile(0, 0, NA - 1)
            with pe.Fori(0, LOOPS, 1) as it:
                IT[0] = it
                for k in range(STEP):
                    step(it * STEP + k, k)
            for u in range(LOOPS * STEP, NU):
                step(u, u % STEP, last=u == NU - 1)

            def spread(c):
                pe.wait_ge(s_ch[c], 16 * (KC * TPC + 1))
                if c >= 2:
                    pe.wait_ge(s_yn, c - 1)
                pe.matmul(ps[:, c % 2, :], sel, rdc[c % 2], start=True, stop=True).then_inc(s_rb, 1)

            def project(c):
                pe.wait_ge(s_yn, c + 1)
                for t in range(TPC):
                    n = c * TPC + t
                    at = TPC - 1 - t if c % 2 else t
                    if n >= 2:
                        pe.wait_ge(s_res, n - 1)
                    for kc in range(KC):
                        mm = pe.matmul(ps[:, 2 + n % 2, 0:C], yTc[c % 3][:, kc, at * P:(at + 1) * P], wo[:, kc, :],
                                       start=kc == 0, stop=kc == KC - 1)
                    mm.then_inc(s_op, 1)

            def route(c):
                pe.wait_ge(s_x1, c + 1)
                if c >= 1:
                    pe.wait_ge(s_x1T, KC * c)
                for kc in range(KC):
                    for t in range(TPC):
                        mm = pe.transpose(ps[:, 4 + kc, t * P:(t + 1) * P],
                                          x_all[:, c * TPC + t, kc * P:(kc + 1) * P], idf)
                    mm.then_inc(s_tp, 1)
                pe.wait_ge(s_x1T, KC * (c + 1))
                for t in range(TPC):
                    n = c * TPC + t
                    for kc in range(KC):
                        mm = pe.matmul(ps[:, 6, n * E:(n + 1) * E], x1T[:, kc, n * P:(n + 1) * P], rt[:, kc, :],
                                       start=kc == 0, stop=kc == KC - 1)
                mm.then_inc(s_lg, 1)

            def gate_up(n):
                c, f = n // FC, n % FC
                if n >= 2:
                    pe.wait_ge(s_h, n - 1)
                for w, bank, done in ((wsg, 0, s_g), (wsu, 1, s_u)):
                    for kc in range(KC):
                        mm = pe.matmul(ps[:, bank + 2 * (n % 2), :], w[:, kc, f * P:(f + 1) * P],
                                       x1T[:, kc, c * CH:(c + 1) * CH], start=kc == 0, stop=kc == KC - 1)
                    mm.then_inc(done, 1)

            def down(c):
                pe.wait_ge(s_h, FC * (c + 1))
                for t in range(TPC):
                    n = c * TPC + t
                    if n >= 2:
                        pe.wait_ge(s_acc, n - 1)
                    for f in range(FC):
                        mm = pe.matmul(ps[:, 4 + n % 2, 0:H], hidden_part(c, f)[:, t * P:(t + 1) * P], wsd[:, f, :],
                                       start=f == 0, stop=f == FC - 1)
                    mm.then_inc(s_dn, 1)

            def rows_T(j, k):
                pe.wait_ge(s_xs[k], (j // 2 + 1) * 16 if isinstance(j, int) else IT[0] * 16 + 32)
                if not isinstance(j, int) or j >= 1:
                    pe.wait_ge(s_ete, j)
                for kc in range(KC):
                    mm = pe.transpose(ps[:, 6, kc * P:(kc + 1) * P], xs[k][:, kc * P:(kc + 1) * P], idf)
                mm.then_inc(s_et, 1)

            pe.wait_ge(s_wo, 32)
            pe.wait_ge(s_yev, 2 * NU + 2)
            spread(0)
            for c in range(NCH):
                if c % 2 == 0:
                    spread(c + 1)
                project(c)
                if c >= 1:
                    route(c - 1)
                if c == 1:
                    spread(2)
            pe.wait_ge(s_wsh, 48)
            gate_up(0)
            route(NCH - 1)

            pe.wait_ge(s_res, NT)
            gate_up(1)
            pe.wait_ge(s_oh, 1)
            flat = oh16[:, :, :].rearrange("p n e -> p (n e)")
            pe.matmul(ps[:, 7, 0:NT * E], tri, flat, start=True, stop=False, skip_group_check=True)
            for n in range(NT - 1):
                later = ps[:, 7, (n + 1) * E:NT * E].rearrange("p (n e) -> p n e", e=E)
                pe.matmul(later, ones, oh16[:, n:n + 1, :].broadcast_to([P, NT - 1 - n, E]), start=False,
                          stop=n == NT - 2, skip_group_check=True)
            for n in range(NT):
                mm = pe.matmul(ps[:, 6, 256:256 + E], ones, oh16[:, n, :], start=n == 0, stop=n == NT - 1)
            mm.then_inc(s_rank, 1)
            gate_up(2)
            gate_up(3)
            for c in range(NCH):
                if c + 1 < NCH:
                    gate_up(FC * (c + 1))
                    gate_up(FC * (c + 1) + 1)
                else:
                    pe.wait_ge(s_slot, 1)
                    rows_T(0, 0)
                    rows_T(1, 1)
                down(c)
                if c + 1 < NCH:
                    gate_up(FC * (c + 1) + 2)
                    gate_up(FC * (c + 1) + 3)

            def expert_up(j, k):
                e = pe.value_load(et[0:1, bass.ds(j, 1)], min_val=0, max_val=E - 1)
                pe.wait_ge(s_ete, j + 1)
                if not isinstance(j, int) or j >= 2:
                    pe.wait_ge(s_eh, j - 1)
                for half_i, done in ((0, s_eg), (1, s_eu)):
                    for kc in range(KC):
                        mm = pe.matmul(ps[:, 2 * k + half_i, :], xsT[k][:, kc, :],
                                       wgu[:, bass.ds(e * (KC * 2 * I) + (kc * 2 * I + half_i * I), I)],
                                       start=kc == 0, stop=kc == KC - 1)
                    mm.then_inc(done, 1)

            def hidden_T(j, k):
                pe.wait_ge(s_eh, j + 1)
                if not isinstance(j, int) or j >= 2:
                    pe.wait_ge(s_ehe, j - 1)
                for f in range(FC):
                    mm = pe.transpose(ps[:, 4 + k, f * P:(f + 1) * P], eh[k][:, f * P:(f + 1) * P], idf)
                mm.then_inc(s_eht, 1)

            def expert_down(j, k):
                e = pe.value_load(et[0:1, bass.ds(j, 1)], min_val=0, max_val=E - 1)
                pe.wait_ge(s_ehe, j + 1)
                if not isinstance(j, int) or j >= 1:
                    pe.wait_ge(s_z, j)
                for f in range(FC):
                    mm = pe.matmul(ps[:, 7, 0:H], ehT[k][:, f, :], wdn[:, bass.ds(e * (FC * H) + f * H, H)],
                                   start=f == 0, stop=f == FC - 1)
                mm.then_inc(s_ed, 1)

            def expert_step(j, k):
                hidden_T(j, k)
                if not isinstance(j, int) or j + 2 < MT:
                    rows_T(j + 2, k)
                if not isinstance(j, int) or j + 1 < MT:
                    expert_up(j + 1, 1 - k)
                expert_down(j, k)

            pe.wait_ge(s_wgu, 16 * E)
            pe.wait_ge(s_wdn, 16 * E)
            expert_up(0, 0)
            pe.wait_ge(s_acc, NT)
            for j in range(2):
                expert_step(j, j)
            with pe.Fori(1, (MT - 3) // 2, 1) as it:
                IT[0] = it
                for k in range(2):
                    expert_step(it * 2 + k, k)
            for j in range(MT - 3, MT):
                expert_step(j, j % 2)

        @block.scalar
        def _(act):
            def put_values(c):
                act.wait_ge(s_vps, c + 1)
                b = c // 2
                for t in range(TPC):
                    kb = (c % 2) * TPC + t
                    ins = act.activation(V_all[:, b * NG:(b + 1) * NG, kb, 0:D],
                                         ps[:, 3, t * NG * D:(t + 1) * NG * D].rearrange("p (g d) -> p g d", g=NG),
                                         ACT.Copy)
                ins.then_inc(s_vev, 1)

            later_loads = [(x_all[:], x_d, s_x), (wo[:], wo_d, s_wo), (rt[:], rt_d, s_wo), (wsg[:], sg_d, s_wsh),
                           (wsu[:], su_d, s_wsh), (wsd[:], sd_d, s_wsh)]
            for n in range(NJ):
                c, k = JOBS[n]
                m = P if k < 2 else NG * D
                act.wait_ge(s_prj, n + 1)
                if n >= 3:
                    act.wait_ge(s_pw[n % 3], 16 * (n // 3))
                act.activation(parts0[n % 3][0:m, 0, :], ps[0:m, 4 + n % 4, :], ACT.Copy).then_inc(s_ph, 1)
                i = 2 * (n - FIRST_A - 1)
                for dst, src, done in later_loads[i:i + 2] if i >= 0 else []:
                    act.dma_start(dst, src.rearrange("(k p) n -> p k n", p=P)).then_inc(done, 16)
                if k == 2:
                    if c >= 1:
                        act.wait_ge(s_vps, c)
                    act.activation(vT, ps[NG * D:P, 4 + n % 4, :], ACT.Copy).then_inc(s_vT, 1)
                if n and JOBS[n - 1][1] == 2:
                    put_values(JOBS[n - 1][0])

            def load_gate_up(e):
                act.dma_start(wgu[:, e * KC * 2 * I:(e + 1) * KC * 2 * I].rearrange("p (k n) -> p k n", k=KC),
                              gu_d[e].rearrange("(k p) n -> p k n", p=P)).then_inc(s_wgu, 16)

            def zero_slots():
                act.wait_ge(s_zero, 3)
                xs_t = xs_d.rearrange("(n p) c -> p n c", p=P)
                act.dma_start(xs_t[:, 0:NT, :], rows[:]).then_inc(s_zf, 16)
                act.dma_start(xs_t[:, NT:MT, :], rows[:, 0:MT - NT, :]).then_inc(s_zf, 16)
                act.dma_start(acc_d[NTOK:NTOK + 2, :], rows[0:2, 0, 0:C]).then_inc(s_zf, 16)

            def step(u, k):
                for s in range(GROUPS):
                    if isinstance(u, int) and u == NU - 2 and s < 5:
                        load_gate_up(s)
                    if isinstance(u, int) and u == NU - 1 and s < E - 5:
                        load_gate_up(5 + s)
                    if isinstance(u, int) and u == NU - 1 and s == E - 5:
                        zero_slots()
                    for hb in range(2):
                        act.wait_ge(s_st, u * (2 * GROUPS) + 2 * s + hb + 1)
                        if hb == 0:
                            act.wait_ge(s_pv, u * GROUPS + s + 1)
                        act.activation(probs[:, 4 * (s % 3) + 2 * hb:4 * (s % 3) + 2 * hb + 2, :],
                                       ps[:, 4 + 2 * hb:6 + 2 * hb, :], ACT.Exp, scale=SCALE).then_inc(s_exp, 1)
                    if s == 4:
                        act.wait_ge(s_pv, u * GROUPS + 4 + 3)
                        act.wait_ge(s_yst[0], u * 16 + 16)
                        act.activation(yU[:, 0, :], ps[:, 2, :], ACT.Copy).then_inc(s_yev, 1)
                act.wait_ge(s_pv, u * GROUPS + GROUPS + 3)
                act.wait_ge(s_yst[1], u * 16 + 16)
                act.activation(yU[:, 1, :], ps[:, 3, :], ACT.Copy).then_inc(s_yev, 1)

            with act.Fori(0, LOOPS, 1) as it:
                for k in range(STEP):
                    step(it * STEP + k, k)
            for u in range(LOOPS * STEP, NU):
                step(u, u % STEP)

            for c in range(NCH):
                for kc in range(KC):
                    act.wait_ge(s_tp, KC * c + kc + 1)
                    act.activation(x1T[:, kc, c * CH:(c + 1) * CH], ps[:, 4 + kc, :], ACT.Copy).then_inc(s_x1T, 1)
            act.wait_ge(s_rt, 2)
            act.activation(score[:], top[:], ACT.Exp, scale=-1.0).then_inc(s_ez, 1)
            for n in range(NCH * FC):
                act.wait_ge(s_g, n + 1)
                if n >= 2:
                    act.wait_ge(s_h, n - 1)
                act.activation(sG[n % 2], ps[:, 2 * (n % 2), :], ACT.Silu).then_inc(s_sg, 1)

            def rows_T(j, k):
                act.wait_ge(s_et, j + 1)
                if not isinstance(j, int) or j >= 2:
                    act.wait_ge(s_eu, j - 1)
                act.activation(xsT[k].rearrange("p k t -> p (k t)"), ps[:, 6, 0:C], ACT.Copy).then_inc(s_ete, 1)
                act.activation(tok[:, bass.ds(j, 1)], xs[k][:, C:C + 1], ACT.Copy).then_inc(s_tok, 1)

            def silu(j, k):
                act.wait_ge(s_eg, j + 1)
                if not isinstance(j, int) or j >= 2:
                    act.wait_ge(s_eh, j - 1)
                act.activation(esG[k], ps[:, 2 * k, :], ACT.Silu).then_inc(s_es, 1)

            def hidden_T(j, k):
                act.wait_ge(s_eht, j + 1)
                if not isinstance(j, int) or j >= 2:
                    act.wait_ge(s_ed, j - 1)
                act.activation(ehT[k].rearrange("p f t -> p (f t)"), ps[:, 4 + k, :], ACT.Copy).then_inc(s_ehe, 1)

            def expert_step(j, k):
                hidden_T(j, k)
                if not isinstance(j, int) or j + 2 < MT:
                    rows_T(j + 2, k)
                if not isinstance(j, int) or j + 1 < MT:
                    silu(j + 1, 1 - k)

            rows_T(0, 0)
            rows_T(1, 1)
            silu(0, 0)
            for j in range(2):
                expert_step(j, j)
            with act.Fori(1, (MT - 3) // 2, 1) as it:
                for k in range(2):
                    expert_step(it * 2 + k, k)
            for j in range(MT - 3, MT):
                expert_step(j, j % 2)

        @block.vector
        def _(dve):
            def reduce_tile(u, t):
                qi, h0, nh, k0, w, second = A_TILES[t]
                dve.wait_ge(s_aps, u * NA + t + 1)
                o = mx1[:, h0:h0 + nh, qi - 4] if second else mx0[:, h0:h0 + nh, qi]
                dve.tensor_reduce(o, ps[:, a_bank(u, t), 0:nh * w].rearrange("p (h w) -> p h w", h=nh), AX.X,
                                  ALU.max).then_inc(s_amax, 1)

            for n in range(NJ):
                m = P if JOBS[n][1] < 2 else NG * D
                h, md, rest = parts0[n % 3][0:m, 0, :], parts0[n % 3][0:m, 1, :], rest0[n % 3][0:m, :]
                dve.wait_ge(s_ph, n + 1)
                if n >= 3:
                    dve.wait_ge(s_pl, n - 2)
                dve.tensor_tensor(rest, ps[0:m, 4 + n % 4, :], h, ALU.subtract).then_inc(s_pr, 1)
                dve.wait_ge(s_pr, n + 1)
                dve.tensor_copy(md, rest).then_inc(s_pm, 1)
                if n >= FIRST_A:
                    for t in first_tiles(n):
                        reduce_tile(0, t)
            dve.wait_ge(s_vev, NCH)
            dve.memset(credit[:, 0:1], 0.0).then_inc(s_exp, 2)
            dve.memset(credit[:, 1:2], 0.0).then_inc(s_pv, 3)
            dve.memset(credit[:, 2:3], 0.0).then_inc(s_yev, 2)
            dve.memset(credit[:, 3:4], 0.0).then_inc(s_yst[0], 16)
            dve.memset(credit[:, 4:5], 0.0).then_inc(s_yst[1], 16)

            def row_max(u):
                first_unit = isinstance(u, int) and u == 0
                if not first_unit:
                    dve.wait_ge(s_mparts, u)
                    for t in range(NA - 1):
                        reduce_tile(u, t)
                dve.wait_ge(s_amax, u * NA + NA - 1)
                dve.tensor_tensor(mx0[:, :, 4:NQ], mx0[:, :, 4:NQ], mx1[:], ALU.max).then_inc(s_split, 1)
                dve.wait_ge(s_split, u * 4 + 1)
                m = mx0[:, :, :].rearrange("p h q -> p (h q)")
                dve.tensor_scalar(mparts[:, 0, :], m, -1.0, None, ALU.mult).then_inc(s_split, 1)
                dve.wait_ge(s_split, u * 4 + 2)
                dve.scalar_tensor_tensor(mrest[:], m, -1.0, mparts[:, 0, :], ALU.mult, ALU.subtract
                                         ).then_inc(s_split, 1)
                dve.wait_ge(s_split, u * 4 + 3)
                dve.tensor_copy(mparts[:, 1, :], mrest[:]).then_inc(s_split, 1)
                dve.wait_ge(s_split, u * 4 + 4)
                dve.tensor_tensor(mparts[:, 2, :], mrest[:], mparts[:, 1, :], ALU.subtract).then_inc(s_mparts, 1)
                dve.wait_ge(s_aps, u * NA + NA)
                if not first_unit:
                    dve.wait_ge(s_mrow, u * 48)
                dve.tensor_copy(mrow[:], ps[0:3 * HG * NQ, a_bank(u, NA - 1), 0:P // 2].bitcast(BF16)
                                ).then_inc(s_amax, 1)

            row_max(0)
            with dve.Fori(0, LOOPS, 1) as it:
                for k in range(STEP):
                    row_max(it * STEP + (k + 1))
            for u in range(LOOPS * STEP, NU - 1):
                row_max(u + 1)

            def invert(b):
                dve.wait_ge(s_den, 16 * (b + 1))
                dve.reciprocal(den[:, b * P:(b + 1) * P], den[:, b * P:(b + 1) * P]).then_inc(s_rd, 1)

            invert(0)

            def normalise(c):
                dve.wait_ge(s_rb, c + 1)
                dve.tensor_tensor(yTc[c % 3], yTc[c % 3], ps[:, c % 2:c % 2 + 1, :].broadcast_to([P, KC, CH]), ALU.mult
                                  ).then_inc(s_yn, 1)

            def residual(c):
                for n in range(c * TPC, (c + 1) * TPC):
                    dve.wait_ge(s_op, n + 1)
                    dve.tensor_tensor(x_all[:, n, :], ps[:, 2 + n % 2, 0:C], x_all[:, n, :], ALU.add).then_inc(s_res, 1)
                    dve.wait_ge(s_res, n + 1)
                    dve.bn_stats(bst[:, n, :], x_all[:, n, :]).then_inc(s_bn, 1)
                for i, n in enumerate(range(c * TPC, (c + 1) * TPC)):
                    dve.wait_ge(s_bn, 2 * TPC * c + i + 1)
                    dve.bn_aggr(mv[:, n, :], bst[:, n, :]).then_inc(s_bn, 1)

            def scale_rows(c):
                for n in range(c * TPC, (c + 1) * TPC):
                    ins = dve.tensor_scalar(x_all[:, n, :], x_all[:, n, :], mv[:, n, 0:1], rstd[:, n:n + 1],
                                            ALU.subtract, ALU.mult)
                return ins

            dve.wait_ge(s_x, 16)
            normalise(0)
            for c in range(NCH):
                if c % 2 == 0:
                    normalise(c + 1)
                residual(c)
                if c == 0:
                    invert(1)
                if c == 1:
                    normalise(2)
                dve.wait_ge(s_rstd, c + 1)
                scale_rows(c).then_inc(s_x1, 1)

            count = [0]

            def chain(ins):
                count[0] += 1
                ins.then_inc(s_rt, 1)
                dve.wait_ge(s_rt, count[0])

            def over_e(ap):
                return ap.rearrange("p (n o) -> p n o", o=1).broadcast_to([P, NT, E])

            iota = cf[:, CF_IOTA:CF_IOTA + E].rearrange("p (o e) -> p o e", o=1).broadcast_to([P, NT, E])
            dve.wait_ge(s_lg, NCH)
            chain(dve.tensor_copy(lg[:, :, :].rearrange("p n e -> p (n e)"), ps[:, 6, 0:NT * E]))
            chain(dve.tensor_reduce(top[:], lg[:], AX.X, ALU.max))
            chain(dve.tensor_tensor(eq[:], lg[:], over_e(top[:]), ALU.is_equal))
            chain(dve.tensor_tensor(eq[:], eq[:], iota, ALU.mult))
            chain(dve.tensor_reduce(first[:], eq[:], AX.X, ALU.min))
            chain(dve.tensor_tensor(oh[:], iota, over_e(first[:]), ALU.is_equal))
            dve.tensor_copy(oh16[:], oh[:]).then_inc(s_oh, 1)
            dve.wait_ge(s_ez, 1)
            chain(dve.tensor_scalar(score[:], score[:], 1.0, None, ALU.add))
            dve.reciprocal(score[:], score[:]).then_inc(s_score, 1)
            def hidden(n):
                c, f = n // FC, n % FC
                dve.wait_ge(s_sg, n + 1)
                dve.wait_ge(s_u, n + 1)
                if f == 0 and c >= 2:
                    dve.wait_ge(s_dn, TPC * (c - 1))
                elif f >= 1 and c >= 1:
                    dve.wait_ge(s_dn, TPC * c)
                dve.tensor_tensor(hidden_part(c, f), sG[n % 2], ps[:, 2 * (n % 2) + 1, :], ALU.mult).then_inc(s_h, 1)

            for n in range(2):
                hidden(n)
            dve.wait_ge(s_rank, 1)
            chain(dve.tensor_copy(cnt[:], ps[:, 6, 256:256 + E]))
            chain(dve.tensor_tensor(many[:], cnt[:, :].rearrange("p (e o) -> p e o", o=1).broadcast_to([P, E, NT]),
                                    cf[:, CF_THR:CF_THR + E * NT].rearrange("p (e n) -> p e n", e=E), ALU.is_gt))
            chain(dve.tensor_reduce(cnt[:], many[:], AX.X, ALU.add))
            chain(dve.tensor_tensor(cum[:], cnt[:, :].rearrange("p (o e) -> p o e", o=1).broadcast_to([P, E, E]),
                                    cf[:, CF_LE:CF_LE + E * E].rearrange("p (a b) -> p a b", a=E), ALU.mult))
            chain(dve.tensor_reduce(end[:], cum[:], AX.X, ALU.add))
            chain(dve.tensor_tensor(start[:], end[:], cnt[:], ALU.subtract))
            chain(dve.tensor_scalar(start[:], start[:], float(P), None, ALU.mult))
            chain(dve.tensor_tensor(place[:], ps[:, 7, 0:NT * E].rearrange("p (n e) -> p n e", e=E),
                                    start[:, :].rearrange("p (o e) -> p o e", o=1).broadcast_to([P, NT, E]), ALU.add))
            chain(dve.tensor_tensor(place[:], place[:], oh[:], ALU.mult))
            chain(dve.tensor_reduce(slotf[:], place[:], AX.X, ALU.add))
            chain(dve.tensor_copy(slot[:], slotf[:]))
            chain(dve.tensor_tensor(after[:], cf[:, CF_J:CF_J + MT * E].rearrange("p (j e) -> p j e", e=E),
                                    end[:, :].rearrange("p (o e) -> p o e", o=1).broadcast_to([P, MT, E]), ALU.is_ge))
            chain(dve.tensor_reduce(etf[:], after[:], AX.X, ALU.add))
            chain(dve.tensor_scalar(etf[:], etf[:], float(E - 1), None, ALU.min))
            dve.tensor_copy(et[:], etf[:]).then_inc(s_slot, 1)

            for n in range(2, FC):
                hidden(n)
            for c in range(NCH):
                if c + 1 < NCH:
                    hidden(FC * (c + 1))
                for n in range(c * TPC, (c + 1) * TPC):
                    dve.wait_ge(s_dn, n + 1)
                    dve.wait_ge(s_xsc, n + 2)
                    dve.tensor_tensor(x_all[:, n, :], ps[:, 4 + n % 2, 0:H], x_all[:, n, :], ALU.add).then_inc(s_acc, 1)
                if c + 1 < NCH:
                    for n in range(1, FC):
                        hidden(FC * (c + 1) + n)

            def hidden_rows(j, k):
                dve.wait_ge(s_es, j + 1)
                dve.wait_ge(s_eu, j + 1)
                if not isinstance(j, int) or j >= 2:
                    dve.wait_ge(s_eht, j - 1)
                dve.tensor_tensor(eh[k], esG[k], ps[:, 2 * k + 1, :], ALU.mult).then_inc(s_eh, 1)

            def finish(j, k):
                dve.wait_ge(s_ed, j + 1)
                dve.wait_ge(s_zin[k], (j // 2 + 1) * 16 if isinstance(j, int) else IT[0] * 16 + 16)
                dve.tensor_tensor(z[k], ps[:, 7, 0:H], z[k], ALU.add).then_inc(s_z, 1)
                dve.wait_ge(s_z, j + 1)
                dve.bn_stats(zst[k][:], z[k]).then_inc(s_zst, 1)
                dve.wait_ge(s_zst, j + 1)
                dve.sem_inc(s_vseen, 1)
                dve.bn_aggr(zmv[k][:], zst[k][:]).then_inc(s_zmv, 1)
                dve.wait_ge(s_zmv, j + 1)
                dve.wait_ge(s_zrs, 2 * j + 2)
                dve.tensor_scalar(z[k], z[k], zmv[k][:, 0:1], zrs[k][:], ALU.subtract, ALU.mult).then_inc(s_fin, 1)

            def expert_step(j, k):
                if not isinstance(j, int) or j + 1 < MT:
                    hidden_rows(j + 1, 1 - k)
                finish(j, k)

            IT = [None]
            hidden_rows(0, 0)
            for j in range(2):
                expert_step(j, j)
            with dve.Fori(1, (MT - 3) // 2, 1) as it:
                IT[0] = it
                for k in range(2):
                    expert_step(it * 2 + k, k)
            for j in range(MT - 3, MT):
                expert_step(j, j % 2)

        @block.gpsimd
        def _(pool):
            pool.memset(V_all[:, :, :, D:VW], 1.0).then_inc(s_vinit, 1)
            pool.memset(Vs[:], 0.0).then_inc(s_vinit, 1)
            pool.memset(rows[:, :, 0:C], 0.0).then_inc(s_zero, 1)
            for i in range(2):
                pool.memset(rows[:, i::2, C:C + 1], float(NTOK + i)).then_inc(s_zero, 1)
            pool.memset(half[:], -0.5).then_inc(s_half, 1)
            for n in range(NJ):
                m = P if JOBS[n][1] < 2 else NG * D
                pool.wait_ge(s_pm, n + 1)
                pool.tensor_tensor(parts0[n % 3][0:m, 2, :], rest0[n % 3][0:m, :], parts0[n % 3][0:m, 1, :],
                                   ALU.subtract).then_inc(s_pl, 1)
            pool.wait_ge(s_vinit, 2)
            pool.wait_ge(s_vev, NCH)

            def values(u, k):
                pool.tensor_copy(Vs[:, k, :, 0:VW], V_all[:, bass.ds(u, 1), :, :].rearrange("p o n d -> p (o n) d")
                                 ).then_inc(s_vs, 1)

            for u in range(2):
                values(u, u)
            with pool.Fori(0, LOOPS, 1) as it:
                for k in range(STEP):
                    pool.wait_ge(s_pv, it * (STEP * GROUPS) + (k * GROUPS + 3))
                    values(it * STEP + (k + 2), (k + 2) % STEP)

            def inverse_root(c, done, value, out_sem, n_out):
                v = slice(c * TPC, (c + 1) * TPC)
                pool.wait_ge(done, value)
                pool.tensor_scalar(rstd[:, v], mv[:, v, 1], EPS, None, ALU.add).then_inc(s_half, 1)
                pool.wait_ge(s_half, n_out)
                pool.tensor_tensor(rstd[:, v], rstd[:, v], half[:, v], ALU.pow).then_inc(out_sem, 1)

            for c in range(NCH):
                inverse_root(c, s_bn, 2 * TPC * (c + 1), s_rstd, c + 2)

            pool.wait_ge(s_slot, 1)
            pool.wait_ge(s_score, 1)
            pool.wait_ge(s_zf, 48)
            pool.tensor_copy(rows[:, :, C], cf[:, CF_TOK:CF_TOK + NT]).then_inc(s_xsc, 1)
            for n in range(NT):
                pool.tensor_scalar(rows[:, n, 0:C], x_all[:, n, :], score[:, n:n + 1], None, ALU.mult
                                   ).then_inc(s_xsc, 1)
            for n in range(NT):
                pool.wait_ge(s_xsc, n + 2)
                pool.indirect_dma_start(xs_d, bass.IndirectOffsetOnAxis(ap=slot[:, n:n + 1], axis=0), rows[:, n, :],
                                        None).then_inc(s_sc, 16)
            pool.wait_ge(s_sc, 16 * NT)
            pool.wait_ge(s_accd, 16 * NCH)

            def wait_for(sem, value):
                pool.wait_ge(sem, value)
                pool.sem_inc(s_pseen, 1)

            def fetch(j, k):
                wait_for(s_tok, j + 1)
                pool.tensor_copy(tokj[k][:], tok[:, bass.ds(j, 1)]).then_inc(s_tokj, 1)
                wait_for(s_tokj, j + 1)
                pool.indirect_dma_start(z[k], None, acc_d, bass.IndirectOffsetOnAxis(ap=tokj[k][:], axis=0)
                                        ).then_inc(s_zin[k], 16)

            def finish(j, k):
                wait_for(s_zmv, j + 1)
                pool.tensor_scalar(zrs[k][:], zmv[k][:, 1:2], EPS, None, ALU.add).then_inc(s_zrs, 1)
                pool.wait_ge(s_zrs, 2 * j + 1)
                pool.tensor_tensor(zrs[k][:], zrs[k][:], half[:, 0:1], ALU.pow).then_inc(s_zrs, 1)
                wait_for(s_fin, j + 1)
                pool.indirect_dma_start(out_d, bass.IndirectOffsetOnAxis(ap=tokj[k][:], axis=0), z[k], None
                                        ).then_inc(s_out[k], 16)

            def expert_step(j, k):
                finish(j, k)
                if not isinstance(j, int) or j + 2 < MT:
                    wait_for(s_out[k], (j // 2 + 1) * 16 if isinstance(j, int) else IT[0] * 16 + 16)
                    fetch(j + 2, k)

            IT = [None]
            for j in range(2):
                fetch(j, j)
            for j in range(2):
                expert_step(j, j)
            with pool.Fori(1, (MT - 3) // 2, 1) as it:
                IT[0] = it
                for k in range(2):
                    expert_step(it * 2 + k, k)
            for j in range(MT - 3, MT):
                expert_step(j, j % 2)


def constants():
    bf16 = mybir.dt.np(BF16)
    import numpy as np
    cf = np.zeros((P, CF_N), np.float32)
    cf[:, CF_ID:CF_ID + P] = np.eye(P)
    cf[0:NH, CF_SEL:CF_SEL + P] = np.arange(P)[None, :] % NH == np.arange(NH)[:, None]
    cf[:, CF_IOTA:CF_IOTA + E] = np.arange(E) - E
    cf[:, CF_THR:CF_THR + E * NT] = np.tile(np.arange(NT) * P, E)
    cf[:, CF_LE:CF_LE + E * E] = (np.arange(E)[None, :] <= np.arange(E)[:, None]).ravel()
    cf[:, CF_J:CF_J + MT * E] = np.repeat(np.arange(MT), E)
    cf[:, CF_TOK:CF_TOK + NT] = np.arange(NT)[None, :] * P + np.arange(P)[:, None]
    big = -3e38
    a = np.arange(P)
    cb = np.zeros((P, CB_N), np.float32)
    cb[:, CB_ID:CB_ID + P] = np.eye(P)
    cb[:, CB_MQK:CB_MQK + P] = np.where(a[None, :] > a[:, None], big, 0)
    cb[:, CB_MKQ:CB_MKQ + HG * P] = np.tile(np.where(a[:, None] > a[None, :], big, 0), (1, HG))
    cb[:, CB_TRI:CB_TRI + P] = a[:, None] < a[None, :]
    cb[:, CB_ONE:CB_ONE + P] = 1
    cb = cb.astype(bf16)
    base = 2.0 ** (-2.0 ** -1)
    slopes = np.array([base * base ** i for i in range(NG)], np.float32).astype(np.float64)
    rest = np.arange(T)[None, :] * slopes[:, None] / SCALE
    al = np.zeros((NG, AL_ROWS, T), bf16)
    for p in range(AL_ROWS):
        al[:, p] = rest.astype(bf16)
        rest = rest - al[:, p].astype(np.float64)
    al = np.concatenate([al.reshape(NG * AL_ROWS, T)] * B)
    one = np.ones((AL_ROWS, HG * T), bf16)
    zero = np.zeros((M_ROWS, HG * T), bf16)
    return {"cf": cf, "cb": cb, "al": al, "one": one, "zero": zero}


def kernel(L0_attn_x, L0_attn_Wq, L0_attn_Wk, L0_attn_Wv, L0_attn_Wo, L0_ffn_router_w, L0_ffn_gate_up_proj,
           L0_ffn_down_proj, L0_ffn_shared_gate_w, L0_ffn_shared_up_w, L0_ffn_shared_down_w):
    import numpy as np
    import concourse.bacc as bacc
    from concourse.bass_utils import run_bass_kernel_spmd
    x = np.ascontiguousarray(L0_attn_x).reshape(NTOK, C)
    arrays = {
        "x": x, "xT": np.ascontiguousarray(x.T), "wq": L0_attn_Wq, "wk": L0_attn_Wk, "wv": L0_attn_Wv,
        "wo": np.asarray(L0_attn_Wo).reshape(NH, D, C).transpose(1, 0, 2).reshape(NH * D, C),
        "rt": np.ascontiguousarray(np.asarray(L0_ffn_router_w).T),
        "gu": L0_ffn_gate_up_proj,
        "dn": L0_ffn_down_proj, "sg": L0_ffn_shared_gate_w, "su": L0_ffn_shared_up_w, "sd": L0_ffn_shared_down_w,
    }
    arrays = {n: np.ascontiguousarray(a) for n, a in arrays.items()} | constants()
    nc = bacc.Bacc("TRN2", target_bir_lowering=False, num_devices=1)
    aps = [nc.dram_tensor(f"in_{n}", a.shape, mybir.dt.from_np(a.dtype), kind="ExternalInput").ap()
           for n, a in arrays.items()]
    out = nc.dram_tensor("out", (NTOK + 2, C), F32, kind="ExternalOutput").ap()
    layer(nc, *aps, out)
    r = run_bass_kernel_spmd(nc, [{f"in_{n}": a for n, a in arrays.items()}], core_ids=[0])
    return r.results[0]["out"][:NTOK].reshape(B, T, C)
```
